# Optimizing a Trainium2 kernel written in Bass

```python
import numpy as np
import jax
import jax.numpy as jnp

def _softmax(x, axis=-1):
    return jax.nn.softmax(x, axis=axis)
def _gelu(x):
    return jax.nn.gelu(x, approximate=True)
def _silu(x):
    return jax.nn.silu(x)
def _sigmoid(x):
    return jax.nn.sigmoid(x)
def _layernorm(x, axis=-1, eps=1e-5):
    m = jnp.mean(x, axis=axis, keepdims=True)
    v = jnp.var(x, axis=axis, keepdims=True)
    return (x - m) / jnp.sqrt(v + eps)
def _scatter_add(tgt, idx, src, axis=0):
    return tgt.at[idx].add(src)
def _segment_sum(src, seg, n):
    return jax.ops.segment_sum(src, seg, n)

kernel_name = 'mk_conv_preact_d1_conv_nchw256_46dfaa'

def setup_inputs(seed: int = 0):
    np.random.seed(seed)
    _w = jnp.asarray
    def _rec_inputs():
        import jax
        import jax.numpy as jnp
        _gk = jax.random.key(seed)
        x = -0.000125 + 0.9999 * jax.random.normal(jax.random.fold_in(_gk, 1), (8, 256, 128, 128), jnp.float32)
        return x
    x = _rec_inputs()
    def _L0_conv_setup():
        import jax, jax.numpy as jnp
        import numpy as np
        N_FEATS = 256
        N_HEAD = 8
        EPS_LN = 1e-05

        def sine_pos_embed(h, w, num_pos_feats, dtype=jnp.float32):
            eps = 1e-06
            scale = 2.0 * np.pi
            temperature = 10000.0
            y = (jnp.arange(1, h + 1, dtype=dtype) / (h + eps) * scale)[:, None, None]
            x = (jnp.arange(1, w + 1, dtype=dtype) / (w + eps) * scale)[None, :, None]
            dim_t = jnp.arange(num_pos_feats, dtype=dtype)
            dim_t = temperature ** (2.0 * jnp.floor(dim_t / 2.0) / num_pos_feats)

            def interleave(t):
                return jnp.stack((jnp.sin(t[..., 0::2]), jnp.cos(t[..., 1::2])), axis=-1).reshape(t.shape[:-1] + (num_pos_feats,))
            py = jnp.broadcast_to(interleave(y / dim_t), (h, w, num_pos_feats))
            px = jnp.broadcast_to(interleave(x / dim_t), (h, w, num_pos_feats))
            return jnp.concatenate((py, px), axis=-1)

        def _ln(t, g, b, eps=EPS_LN):
            mu = jnp.mean(t, axis=-1, keepdims=True)
            var = jnp.var(t, axis=-1, keepdims=True)
            return (t - mu) * jax.lax.rsqrt(var + eps) * g + b
        key = jax.random.key(seed)
        ks = jax.random.split(key, 4)
        b, c, h, w = (8, N_FEATS, 128, 128)
        d_k = c // N_HEAD
        s = 0.02
        return dict(x=jax.random.normal(ks[0], (b, c, h, w), jnp.float32), Wq=jax.random.normal(ks[1], (c, c), jnp.float32) * s, bq=jnp.zeros((c,), jnp.float32), Wk=jax.random.normal(ks[2], (c, c), jnp.float32) * s, bk=jnp.zeros((c,), jnp.float32), Wv=jax.random.normal(ks[3], (c, c), jnp.float32) * s, bv=jnp.zeros((c,), jnp.float32), gK=jnp.ones((N_HEAD, d_k), jnp.float32), bK=jnp.zeros((N_HEAD, d_k), jnp.float32), gV=jnp.ones((N_HEAD, d_k), jnp.float32), bV=jnp.zeros((N_HEAD, d_k), jnp.float32), g_ln=jnp.ones((c,), jnp.float32), b_ln=jnp.zeros((c,), jnp.float32))
    _L0_conv_all = _L0_conv_setup()
    _L0_conv_in = {k: v for k, v in _L0_conv_all.items() if k in ('Wq', 'bq', 'Wk', 'bk', 'Wv', 'bv', 'gK', 'bK', 'gV', 'bV', 'g_ln', 'b_ln', )}
    del _L0_conv_all

    return {
        "x": x,
        "L0_conv_Wq": _L0_conv_in["Wq"],
        "L0_conv_bq": _L0_conv_in["bq"],
        "L0_conv_Wk": _L0_conv_in["Wk"],
        "L0_conv_bk": _L0_conv_in["bk"],
        "L0_conv_Wv": _L0_conv_in["Wv"],
        "L0_conv_bv": _L0_conv_in["bv"],
        "L0_conv_gK": _L0_conv_in["gK"],
        "L0_conv_bK": _L0_conv_in["bK"],
        "L0_conv_gV": _L0_conv_in["gV"],
        "L0_conv_bV": _L0_conv_in["bV"],
        "L0_conv_g_ln": _L0_conv_in["g_ln"],
        "L0_conv_b_ln": _L0_conv_in["b_ln"],
    }

def reference(x, L0_conv_Wq, L0_conv_bq, L0_conv_Wk, L0_conv_bk, L0_conv_Wv, L0_conv_bv, L0_conv_gK, L0_conv_bK, L0_conv_gV, L0_conv_bV, L0_conv_g_ln, L0_conv_b_ln):
    import jax
    import jax.numpy as jnp
    def _L0_conv_ref(x, Wq, bq, Wk, bk, Wv, bv, gK, bK, gV, bV, g_ln, b_ln):
        import jax, jax.numpy as jnp
        import numpy as np
        N_FEATS = 256
        N_HEAD = 8
        EPS_LN = 1e-05

        def sine_pos_embed(h, w, num_pos_feats, dtype=jnp.float32):
            eps = 1e-06
            scale = 2.0 * np.pi
            temperature = 10000.0
            y = (jnp.arange(1, h + 1, dtype=dtype) / (h + eps) * scale)[:, None, None]
            x = (jnp.arange(1, w + 1, dtype=dtype) / (w + eps) * scale)[None, :, None]
            dim_t = jnp.arange(num_pos_feats, dtype=dtype)
            dim_t = temperature ** (2.0 * jnp.floor(dim_t / 2.0) / num_pos_feats)

            def interleave(t):
                return jnp.stack((jnp.sin(t[..., 0::2]), jnp.cos(t[..., 1::2])), axis=-1).reshape(t.shape[:-1] + (num_pos_feats,))
            py = jnp.broadcast_to(interleave(y / dim_t), (h, w, num_pos_feats))
            px = jnp.broadcast_to(interleave(x / dim_t), (h, w, num_pos_feats))
            return jnp.concatenate((py, px), axis=-1)

        def _ln(t, g, b, eps=EPS_LN):
            mu = jnp.mean(t, axis=-1, keepdims=True)
            var = jnp.var(t, axis=-1, keepdims=True)
            return (t - mu) * jax.lax.rsqrt(var + eps) * g + b
        b, c, h, w = x.shape
        d_k = c // N_HEAD
        n = h * w
        pos = sine_pos_embed(h, w, c // 2, dtype=x.dtype).reshape(1, n, c)
        xs = jnp.transpose(x, (0, 2, 3, 1)).reshape(b, n, c)
        qk_in = xs + pos

        def proj(t, W, bias):
            return (t @ W.T + bias).reshape(b, n, N_HEAD, d_k).transpose(0, 2, 1, 3)
        q = proj(qk_in, Wq, bq)
        k = proj(qk_in, Wk, bk)
        v = proj(xs, Wv, bv)
        k = _ln(k, gK[None, :, None, :], bK[None, :, None, :])
        v = _ln(v, gV[None, :, None, :], bV[None, :, None, :])
        scores = jnp.einsum('bhnd,bhne->bhde', k, v) / n
        out = jnp.einsum('bhnd,bhde->bhne', q, scores)
        out = out.transpose(0, 2, 1, 3).reshape(b, n, c)
        out = out + out
        out = _ln(out, g_ln, b_ln)
        return jnp.transpose(out.reshape(b, h, w, c), (0, 3, 1, 2))

    def _gn(v, G=32, eps=1e-5):
        B_, C_, H_, W_ = v.shape
        g = v.reshape(B_, G, C_ // G, H_, W_)
        m = jnp.mean(g, axis=(2, 3, 4), keepdims=True)
        s = jnp.var(g, axis=(2, 3, 4), keepdims=True)
        return ((g - m) / jnp.sqrt(s + eps)).reshape(v.shape)

    def _ln_c(v, eps=1e-6):
        m = jnp.mean(v, axis=1, keepdims=True)
        s = jnp.var(v, axis=1, keepdims=True)
        return (v - m) / jnp.sqrt(s + eps)

    def _ln_t(v, eps=1e-5):
        m = jnp.mean(v, axis=-1, keepdims=True)
        s = jnp.var(v, axis=-1, keepdims=True)
        return (v - m) / jnp.sqrt(s + eps)

    def _to_tokens(v):
        B_, C_, H_, W_ = v.shape
        return v.reshape(B_, C_, H_ * W_).transpose(0, 2, 1)
    def _from_tokens(t, like):
        B_, C_, H_, W_ = like.shape
        return t.transpose(0, 2, 1).reshape(B_, C_, H_, W_)

    x = x + _L0_conv_ref(_gn(x), L0_conv_Wq, L0_conv_bq, L0_conv_Wk, L0_conv_bk, L0_conv_Wv, L0_conv_bv, L0_conv_gK, L0_conv_bK, L0_conv_gV, L0_conv_bV, L0_conv_g_ln, L0_conv_b_ln)
    return x


_drawn_inputs = setup_inputs


def setup_inputs(seed=0):
    import zlib

    import numpy as np

    out = dict(_drawn_inputs(seed))
    spreads = {'L0_conv_bq': (0.0, 0.1),
     'L0_conv_bk': (0.0, 0.1),
     'L0_conv_bv': (0.0, 0.1),
     'L0_conv_gK': (1.0, 0.2),
     'L0_conv_bK': (0.0, 0.1),
     'L0_conv_gV': (1.0, 0.2),
     'L0_conv_bV': (0.0, 0.1),
     'L0_conv_g_ln': (1.0, 0.2),
     'L0_conv_b_ln': (0.0, 0.1)}
    factors = {}
    for name, (base, spread) in spreads.items():
        noise = np.random.default_rng([zlib.crc32(name.encode()), seed]).standard_normal(out[name].shape)
        drawn = base * np.exp(spread * noise) if base else spread * noise
        out[name] = jnp.asarray(drawn.astype(out[name].dtype))
    for name, factor in factors.items():
        out[name] = (out[name] * factor).astype(out[name].dtype)
    return out
```

```python
from contextlib import ExitStack

import concourse.bass as bass
from concourse import mybir

ALU = mybir.AluOpType
ACT = mybir.ActivationFunctionType
F32 = mybir.dt.float32
F16 = mybir.dt.float16
AX = mybir.AxisListType

P = 128
B = 8
C = 256
CH = C // P
W = 128
ROWS = 128
NPIX = ROWS * W
HEADS = 8
DK = C // HEADS
HPC = HEADS // CH
GTILES = 4
GPIX = GTILES * W
GROUPS = ROWS // GTILES
PAIRS = 2 * GROUPS
UNIT = 2 * GPIX
UNITS = NPIX // UNIT
SPARE = 1
SLOTS = UNITS + SPARE
NUNITS = B * UNITS
HALF = ROWS // 2
EPS = 1e-5
KVR = 4
VROW = C + 1 + C + 1
WBOUND = 64.0
MBOUND = 32768.0

CONSTS = [("ident", P), ("lrot", P), ("lone", P), ("mask", P), ("blk8", P), ("pos", 2 * P), ("sel", HALF), ("ones", P)]
CAT = {}
_at = 0
for _name, _n in CONSTS:
    CAT[_name] = (_at, _at + _n)
    _at += _n
NCONST = _at


def sweep(eng, body, b):
    for g in (0, 1):
        body(b, g, g)
    with eng.Fori(0, (GROUPS - 4) // 2) as i:
        body(b, 2 * i + 2, 0)
        body(b, 2 * i + 3, 1)
    for g in (GROUPS - 2, GROUPS - 1):
        body(b, g, g % 2)


def ends(g):
    return (isinstance(g, int) and g == 0, isinstance(g, int) and g == GROUPS - 1)


def build(nc, x, Wq, bq, Wk, bk, Wv, bv, gK, bK, gV, bV, g_ln, b_ln, consts, y):
    with ExitStack() as ctx:
        def sb(name, shape, dt=F32):
            return ctx.enter_context(nc.sbuf_tensor(name, shape, dt))

        def sem(name):
            return ctx.enter_context(nc.semaphore(name))

        xr = sb("x_ring", [P, SLOTS, CH, UNIT])
        wkv_hi = sb("wkv_hi", [P, CH, 2 * C], F16)
        wkv_lo = sb("wkv_lo", [P, CH, 2 * C], F16)
        rowpart = sb("rowpart", [P, 2, C], F16)
        sel = sb("sel", [P, HALF], F16)
        ones_hl = sb("ones_hl", [P, P], F16)
        kv_add = sb("kv_add", [P, 2 * C])
        cst = sb("cst", [P, NCONST])
        posb = sb("posb", [P, CH, P])
        wql = sb("wql", [P, CH, C])
        bql = sb("bql", [P, CH, P])
        gvm = sb("gvm", [P, CH, P])
        bvm = sb("bvm", [P, CH, P])
        cols = sb("cols", [P, 5, CH])
        sprime = sb("sprime", [P, CH, P])
        m_hi = sb("m_hi", [P, 3, C], F16)
        m_lo = sb("m_lo", [P, 2, C], F16)
        u = [sb(f"u{i}", [P, CH, GPIX]) for i in range(2)]
        hi = [sb(f"hi{i}", [P, CH, GPIX], F16) for i in range(2)]
        lo = [sb(f"lo{i}", [P, CH, GPIX], F16) for i in range(2)]
        kv = [sb(f"kv{i}", [P, 2, VROW]) for i in range(KVR)]
        sq = [sb(f"sq{i}", [P, 2 * 2 * C]) for i in range(2)]
        kaug = [sb(f"kaug{i}", [P, 2, C]) for i in range(2)]
        ssum = sb("ssum", [P, 4, 2 * 2 * HEADS])
        std = sb("std", [P, 4, 2 * 2 * HEADS])
        rstd = sb("rstd", [P, 4, 2 * 2 * HEADS])
        stats = sb("stats", [P, CH, GROUPS, 6])
        obn = sb("obn", [P, 2, GTILES, 6])
        otmp = sb("otmp", [P, 2, 3, GTILES])
        ovar = sb("ovar", [P, 2, GTILES])
        ostd = sb("ostd", [P, 2, GTILES])
        orstd = sb("orstd", [P, 2, GTILES])
        mv = sb("mv", [P, CH, 2])
        gmean = sb("gmean", [P, CH])
        gdev = sb("gdev", [P, CH])
        gsq = sb("gsq", [P, CH])
        gvar = sb("gvar", [P, CH])
        gstd = sb("gstd", [P, CH])
        grstd = sb("grstd", [P, CH])
        gshift = sb("gshift", [P, CH])
        eps = sb("eps", [P, 4])
        small = sb("small", [P, 32])
        max_in = sb("max_in", [P, 8])
        max_all = sb("max_all", [P, 8])
        zero16 = sb("zero16", [P, P + 1], F16)
        mmean = sb("mmean", [P, 4])
        z = [s[:].rearrange("p (t c) -> p t c", t=GTILES) for s in sq]
        wout = [t[:].rearrange("p a b -> p (a b)")[:, 0:CH * GPIX].rearrange("p (c t) -> p c t", c=CH) for t in kv[0:2]]
        flat = xr[:].rearrange("p s c t -> p (s c t)")

        def temp(i, n):
            return flat[:, i * 1024:i * 1024 + n]
        wk_in = temp(0, 2 * C).rearrange("p (j c) -> p j c", j=CH)
        wv_in = temp(1, 2 * C).rearrange("p (j c) -> p j c", j=CH)
        wq_in = temp(2, 2 * C).rearrange("p (j c) -> p j c", j=CH)
        bias_in = temp(3, 2 * C)
        gv_in = temp(4, 2 * C)
        wt = temp(5, 1024).rearrange("p (c d) -> p c d", c=CH)
        wc = temp(6, 1024).rearrange("p (c d) -> p c d", c=CH)
        lmat = temp(7, CH * P).rearrange("p (j d) -> p j d", j=CH)
        lone_g = temp(8, CH * P).rearrange("p (j d) -> p j d", j=CH)
        bias_c = temp(9, 2 * C)
        bq_rep = temp(10, CH * P).rearrange("p (j d) -> p j d", j=CH)
        m_cent = [u[0][:].rearrange("p c t -> p (c t)")[:, 0:3 * C].rearrange("p (m c) -> p m c", m=3)][0]
        s_gain = u[1][:].rearrange("p c t -> p (c t)")[:, 0:CH * P].rearrange("p (j d) -> p j d", j=CH)

        ps = ctx.enter_context(nc.psum_tensor("ps", [P, 8, 512], F32))
        kv_ps = [ps[:, 2 * i:2 * i + 2, :] for i in range(2)]
        o_ps = [ps[:, 2 * i:2 * i + 2, :].rearrange("p a (t c) -> p (a t) c", t=2) for i in range(2)]
        s_ps = [ps[:, 4 + j, 0:P + 1] for j in range(CH)]
        t_ps = [ps[:, 4 + 2 * i:6 + 2 * i, :] for i in range(2)]

        def const(name):
            a, b_ = CAT[name]
            return cst[:, a:b_]
        ident = const("ident")
        pos = const("pos").rearrange("p (c t) -> p c t", c=CH)

        params_loaded = sem("params_loaded")
        loaded = [sem(f"loaded{i}") for i in range(2)]
        stored = [sem(f"stored{i}") for i in range(2)]
        setup_dve = sem("setup_dve")
        setup_pe = sem("setup_pe")
        setup_pool = sem("setup_pool")
        max_ready = sem("max_ready")
        wc_ready = sem("wc_ready")
        lmat_ready = sem("lmat_ready")
        ring_free = sem("ring_free")
        stats_done = sem("stats_done")
        gn_dve = sem("gn_dve")
        gn_pe = sem("gn_pe")
        gn_act = sem("gn_act")
        u_ready = sem("u_ready")
        hi_ready = sem("hi_ready")
        lo_ready = sem("lo_ready")
        kv_proj = sem("kv_proj")
        kv_evac = sem("kv_evac")
        squared = sem("squared")
        summed = sem("summed")
        std_ready = sem("std_ready")
        rstd_ready = sem("rstd_ready")
        k_scaled = sem("k_scaled")
        scored = sem("scored")
        sums_done = sem("sums_done")
        kv_free = sem("kv_free")
        mix_dve = sem("mix_dve")
        mix_pe = sem("mix_pe")
        o_ready = sem("o_ready")
        obn_ready = sem("obn_ready")
        ovar_step = sem("ovar_step")
        ovar_ready = sem("ovar_ready")
        ostd_ready = sem("ostd_ready")
        orstd_ready = sem("orstd_ready")
        z_ready = sem("z_ready")
        t_ready = sem("t_ready")
        w_ready = sem("w_ready")
        y_ready = sem("y_ready")

        x_dram = x.rearrange("b (c p) (k r) w -> b k p c (r w)", p=P, k=UNITS)
        y_dram = y.rearrange("b (c p) (k r) w -> b k p c (r w)", p=P, k=UNITS)

        def slot(n):
            return n % SLOTS

        def x_group(b, g, parity):
            s = slot(UNITS * b + (g - parity) // 2)
            t = slice(parity * GPIX, (parity + 1) * GPIX)
            if isinstance(s, int):
                return xr[:, s, :, t]
            return xr[:, bass.ds(s, 1), :, t].rearrange("p a c t -> p (a c) t")

        def wait_parts_free(eng, b, phase, g):
            if phase == 0:
                if not (isinstance(g, int) and g < 2):
                    eng.wait_ge(kv_proj, PAIRS * b + 2 * g - 2)
            elif isinstance(g, int) and g < 2:
                eng.wait_ge(kv_proj, PAIRS * b + PAIRS)
            else:
                eng.wait_ge(o_ready, GROUPS * b + g - 1)

        block = ctx.enter_context(nc.Block())

        @block.sync
        def _(sp):
            def load(n, par):
                if not isinstance(n, int) or n >= 2:
                    sp.wait_ge(loaded[par], (n - par) // 2 * 16)
                s = slot(n)
                if isinstance(n, int):
                    sp.dma_start(xr[:, s, :, :], x_dram[n // UNITS, n % UNITS]).then_inc(loaded[par], 16)
                else:
                    sp.dma_start(xr[:, bass.ds(s, 1), :, :].rearrange("p a c t -> p (a c) t"),
                                 x_dram[bass.ds(n // UNITS, 1), bass.ds(n % UNITS, 1)].rearrange("a k p c t -> p (a k c) t")
                                 ).then_inc(loaded[par], 16)

            def store(m, par):
                sp.wait_ge(y_ready, 2 * m + 2)
                s = slot(m)
                if isinstance(m, int):
                    sp.dma_start(y_dram[m // UNITS, m % UNITS], xr[:, s, :, :]).then_inc(stored[par], 16)
                else:
                    sp.dma_start(y_dram[bass.ds(m // UNITS, 1), bass.ds(m % UNITS, 1)].rearrange("a k p c t -> p (a k c) t"),
                                 xr[:, bass.ds(s, 1), :, :].rearrange("p a c t -> p (a c) t")
                                 ).then_inc(stored[par], 16)

            def store_and_refill(m, par):
                store(m, par)
                sp.wait_ge(stored[1 - par], ((m - 1) // 2 + 1) * 16 if isinstance(m, int) else
                           ((m - 1 - (1 - par)) // 2) * 16 + 16)
                load(m - 1 + SLOTS, (par - 1 + SLOTS) % 2)

            sp.dma_start(cst[:], consts).then_inc(params_loaded, 16)
            for dst, src in ((wk_in, Wk), (wv_in, Wv), (wq_in, Wq)):
                sp.dma_start(dst, src.rearrange("(j p) c -> p j c", p=P)).then_inc(params_loaded, 16)
            for i, src in enumerate((bk, bv)):
                sp.dma_start(bias_in[:, i * C:(i + 1) * C], src.rearrange("(a c) -> a c", a=1).partition_broadcast(P)
                             ).then_inc(params_loaded, 16)
            for i, src in enumerate((gV, bV)):
                sp.dma_start(gv_in[:, i * C:(i + 1) * C],
                             src.rearrange("h d -> (h d)").rearrange("(a c) -> a c", a=1).partition_broadcast(P)
                             ).then_inc(params_loaded, 16)
            for i, src in enumerate((gK.rearrange("h d -> (h d)"), bK.rearrange("h d -> (h d)"), bq, g_ln, b_ln)):
                sp.dma_start(cols[:, i, :], src.rearrange("(j p) -> p j", p=P), allow_slow_non_contiguous=True
                             ).then_inc(params_loaded, 16)
            sp.wait_ge(ring_free, 1)
            for n in range(SLOTS):
                load(n, n % 2)
            store(0, 0)
            steps = NUNITS - SLOTS
            with sp.Fori(0, steps // 2) as i:
                store_and_refill(2 * i + 1, 1)
                store_and_refill(2 * i + 2, 0)
            for m in range(steps // 2 * 2 + 1, steps + 1):
                store_and_refill(m, m % 2)
            for m in range(steps + 1, NUNITS):
                store(m, m % 2)
            sp.wait_ge(stored[0], NUNITS // 2 * 16)
            sp.wait_ge(stored[1], NUNITS // 2 * 16)

        @block.vector
        def _(dve):
            step = [0]

            def link(ins):
                step[0] += 1
                ins.then_inc(setup_dve, 1)
                dve.wait_ge(setup_dve, step[0])
            dve.wait_ge(params_loaded, 16 * 13)
            dve.tensor_copy(sel[:], const("sel"))
            dve.tensor_copy(ones_hl[:], const("ones"))
            dve.memset(m_hi[:], 0.0)
            dve.memset(zero16[:], 0.0)
            for t in kaug:
                dve.memset(t[:], 1.0)
            for t in kv:
                ins = dve.memset(t[:], 1.0)
            ins.then_inc(kv_free, 1)
            dve.memset(eps[:], EPS)
            dve.wait_ge(setup_pe, 1)
            link(dve.tensor_copy(wt, ps[:, 0:CH, :]))
            wt_h = wt.rearrange("p c (h d) -> p c h d", d=DK)
            hm = small[:, 0:32].rearrange("p (c h) -> p c h", c=CH)
            link(dve.tensor_reduce(hm, wt_h, AX.X, ALU.add))
            link(dve.tensor_scalar(small[:, 0:32], small[:, 0:32], -1.0 / DK, None, ALU.mult))
            for c in range(CH):
                ins = dve.tensor_tensor(wc[:, c, :].rearrange("p (h d) -> p h d", d=DK), wt_h[:, c],
                                        hm[:, c, :].unsqueeze(2).broadcast_to([P, 16, DK]), ALU.add)
            link(ins)
            bias_h = bias_in.rearrange("p (h d) -> p h d", d=DK)
            link(dve.tensor_reduce(small[:, 0:16], bias_h, AX.X, ALU.add))
            link(dve.tensor_scalar(small[:, 0:16], small[:, 0:16], -1.0 / DK, None, ALU.mult))
            link(dve.tensor_tensor(bias_c.rearrange("p (h d) -> p h d", d=DK), bias_h,
                                   small[:, 0:16].unsqueeze(2).broadcast_to([P, 16, DK]), ALU.add))
            link(dve.memset(small[:], 0.0))

            def absmax(col, src):
                return dve.tensor_reduce(small[:, col:col + 1], src, AX.XY, ALU.max, apply_absolute_value=True)
            absmax(0, wc)
            absmax(1, wq_in)
            for col, src in ((2, cols[:, 0:1, :]), (3, cols[:, 1:2, :]), (6, cols[:, 2:3, :])):
                absmax(col, src)
            absmax(4, gv_in[:, 0:C].rearrange("p (a c) -> p a c", a=1))
            link(absmax(5, gv_in[:, C:2 * C].rearrange("p (a c) -> p a c", a=1)))
            link(dve.tensor_tensor(small[:, 1:2], small[:, 1:2], small[:, 6:7], ALU.max))
            dve.tensor_copy(max_in[:], small[:, 0:8]).then_inc(max_ready, 1)
            dve.wait_ge(setup_pool, 1)
            link(dve.tensor_scalar(small[:, 8:16], max_all[:], 1e-12, None, ALU.max))
            link(dve.scalar_tensor_tensor(small[:, 16:17], small[:, 10:11], float(DK) ** 0.5, small[:, 11:12], ALU.mult, ALU.add))
            link(dve.scalar_tensor_tensor(small[:, 17:18], small[:, 12:13], float(DK) ** 0.5, small[:, 13:14], ALU.mult, ALU.add))
            link(dve.tensor_scalar(small[:, 16:18], small[:, 16:18], 1e-3, None, ALU.max))
            link(dve.tensor_tensor(small[:, 18:19], small[:, 16:17], small[:, 17:18], ALU.mult))
            link(dve.tensor_tensor(small[:, 19:20], small[:, 18:19], small[:, 9:10], ALU.mult))
            link(dve.reciprocal(small[:, 20:21], small[:, 8:9]))
            link(dve.reciprocal(small[:, 21:22], small[:, 19:20]))
            link(dve.tensor_scalar(small[:, 22:23], small[:, 20:21], WBOUND, None, ALU.mult))
            link(dve.tensor_scalar(small[:, 23:24], small[:, 21:22], MBOUND / (2 * DK), None, ALU.mult))
            link(dve.tensor_scalar(small[:, 24:25], small[:, 23:24], 1.0 / NPIX, None, ALU.mult))
            link(dve.tensor_scalar(eps[:, 1:2], small[:, 22:23], small[:, 22:23], EPS, ALU.mult, ALU.mult))
            link(dve.tensor_scalar(eps[:, 2:3], small[:, 23:24], small[:, 23:24], EPS / 4, ALU.mult, ALU.mult))
            link(dve.tensor_scalar(wc, wc, small[:, 22:23], None, ALU.mult))
            link(dve.tensor_scalar(bias_c, bias_c, small[:, 22:23], None, ALU.mult))
            dve.tensor_copy(wkv_hi[:], wc).then_inc(wc_ready, 1)
            dve.wait_ge(wc_ready, 1)
            link(dve.tensor_tensor(wkv_lo[:], wc, wkv_hi[:], ALU.subtract))
            for j in range(CH):
                ins = dve.tensor_scalar(lone_g[:, j, :], const("lone"), cols[:, 1, j:j + 1], None, ALU.mult)
            link(ins)
            for j in range(CH):
                dve.scalar_tensor_tensor(lmat[:, j, :], const("lrot"), cols[:, 0, j:j + 1], lone_g[:, j, :], ALU.mult, ALU.add)
            for j in range(CH):
                dve.tensor_copy(bq_rep[:, j, :], cols[:, 2, j:j + 1].broadcast_to([P, P]))
                for t, o in ((gvm, 0), (bvm, C)):
                    ins = dve.tensor_tensor(t[:, j, :], gv_in[:, o + j * P:o + (j + 1) * P], const("mask"), ALU.mult)
            ins.then_inc(lmat_ready, 1)
            dve.wait_ge(setup_pe, 2)
            dve.tensor_tensor(kv_add[:, 0:C], ps[:, 2, 0:C], bias_c[:, 0:C], ALU.add)
            dve.tensor_copy(kv_add[:, C:2 * C], bias_c[:, C:2 * C])
            for h in range(2):
                dve.tensor_copy(rowpart[0:HALF, h, :], ps[0:HALF, 3 + h, 0:C])
                link(dve.tensor_copy(sq[0][HALF:P, h * C:h * C + C // 2].bitcast(F16), ps[HALF:P, 3 + h, 0:C]))
                link(dve.tensor_tensor(rowpart[HALF:P, h, :], ps[HALF:P, 3 + h, 0:C],
                                       sq[0][HALF:P, h * C:h * C + C // 2].bitcast(F16), ALU.subtract))
            dve.wait_ge(setup_pe, 3)
            for j in range(CH):
                dve.tensor_scalar(wql[:, j, :], ps[:, 5 + j, 0:C], small[:, 24:25], None, ALU.mult)
                ins = dve.tensor_scalar(bql[:, j, :], ps[:, 5 + j, C:C + P], small[:, 24:25], None, ALU.mult)
            link(ins)
            dve.drain().then_inc(ring_free, 1)

            def unit_stats(b, k, par):
                n = UNITS * b + k
                dve.wait_ge(loaded[par], (n - par) // 2 * 16 + 16)
                for h in range(2):
                    xg = x_group(b, 2 * k + h, h)
                    for c in range(CH):
                        if isinstance(k, int):
                            dst = stats[:, c, 2 * k + h, :]
                        else:
                            dst = stats[:, c, bass.ds(2 * k + h, 1), :].rearrange("p a s -> p (a s)")
                        ins = dve.bn_stats(dst, xg[:, c, :])
                ins.then_inc(stats_done, 1)

            def group_norm(b):
                G = 8
                dve.wait_ge(stats_done, UNITS * b + UNITS)
                dve.memset(mmean[:, 3:4], 0.0)
                for c in range(CH):
                    ins = dve.bn_aggr(mv[:, c, :], stats[:, c].rearrange("p g s -> p (g s)"))
                ins.then_inc(gn_dve, 1)
                dve.wait_ge(gn_pe, 2 * b + 1)
                dve.tensor_copy(gmean[:], ps[:, 0, 0:CH]).then_inc(gn_dve, 1)
                dve.wait_ge(gn_dve, G * b + 2)
                dve.tensor_tensor(gdev[:], mv[:, :, 0], gmean[:], ALU.subtract).then_inc(gn_dve, 1)
                dve.wait_ge(gn_dve, G * b + 3)
                dve.tensor_tensor(gsq[:], gdev[:], gdev[:], ALU.mult).then_inc(gn_dve, 1)
                dve.wait_ge(gn_dve, G * b + 4)
                dve.tensor_tensor(gvar[:], gsq[:], mv[:, :, 1], ALU.add).then_inc(gn_dve, 1)
                dve.wait_ge(gn_act, b + 1)
                dve.reciprocal(grstd[:], gstd[:]).then_inc(gn_dve, 1)
                dve.wait_ge(gn_dve, G * b + 6)

            def group_shift(b):
                G = 8
                dve.scalar_tensor_tensor(gshift[:], gmean[:], -1.0, grstd[:], ALU.mult, ALU.mult).then_inc(gn_dve, 1)
                dve.wait_ge(kv_free, b + 1)
                dve.wait_ge(gn_dve, G * b + 7)
                for c in range(CH):
                    ins = dve.tensor_scalar(posb[:, c, :], pos[:, c, :], gshift[:, c:c + 1], None, ALU.add)
                ins.then_inc(gn_dve, 1)
                dve.wait_ge(gn_dve, G * b + 8)

            def normalise(b, g, par):
                H = 2 * GROUPS * b + g
                if not (isinstance(g, int) and g < 2):
                    dve.wait_ge(hi_ready, H - 1)
                xg = x_group(b, g, par)
                for c in range(CH):
                    ins = dve.tensor_scalar(u[par][:, c, :], xg[:, c, :], gmean[:, c:c + 1], grstd[:, c:c + 1],
                                            ALU.subtract, ALU.mult)
                ins.then_inc(u_ready, 1)

            def low_part(b, g, par):
                H = 2 * GROUPS * b + g
                dve.wait_ge(hi_ready, H + 1)
                wait_parts_free(dve, b, 0, g)
                dve.tensor_tensor(lo[par][:], u[par][:], hi[par][:], ALU.subtract).then_inc(lo_ready, 1)

            def evacuate(b, p, q):
                Pn = PAIRS * b + p
                dve.wait_ge(kv_proj, Pn + 1)
                if not (isinstance(p, int) and p < KVR):
                    dve.wait_ge(scored, Pn - KVR + 1)
                for t in range(2):
                    src = kv_ps[q % 2][:, t, :].rearrange("p (a c) -> p a c", a=2)
                    dst = kv[q][:, t, :].rearrange("p (a c) -> p a c", a=2)[:, :, 0:C]
                    add = kv_add[:].rearrange("p (a c) -> p a c", a=2)
                    ins = dve.tensor_tensor(dst, src, add, ALU.add)
                ins.then_inc(kv_evac, 1)

            def sum_squares(b, p, q):
                Pn = PAIRS * b + p
                dve.wait_ge(squared, Pn + 1)
                dve.tensor_reduce(ssum[:, q, :], sq[q % 2][:].rearrange("p (h d) -> p h d", d=DK),
                                  AX.X, ALU.add).then_inc(summed, 1)

            def inverse_std(b, p, q):
                Pn = PAIRS * b + p
                dve.wait_ge(std_ready, Pn + 1)
                dve.reciprocal(rstd[:, q, :], std[:, q, :]).then_inc(rstd_ready, 1)

            def phase1_group(b, g, par):
                p, q = 2 * g, 2 * par
                first, last = ends(g)
                if not last:
                    normalise(b, g + 1, 1 - par)
                evacuate(b, p, q)
                if not first:
                    inverse_std(b, p - 2, (q + 2) % 4)
                if not last:
                    low_part(b, g + 1, 1 - par)
                if not first:
                    sum_squares(b, p - 1, (q + 3) % 4)
                evacuate(b, p + 1, q + 1)
                if not first:
                    inverse_std(b, p - 1, (q + 3) % 4)
                sum_squares(b, p, q)

            def mix(b):
                N = 6
                dve.wait_ge(sums_done, b + 1)
                for j in range(CH):
                    v0, one = (1, 0) if j == 0 else (0, P)
                    dve.tensor_tensor(s_gain[:, j, :], s_ps[j][:, v0:v0 + P], gvm[:, j, :], ALU.mult)
                    ins = dve.tensor_copy(mmean[:, j:j + 1], s_ps[j][:, one:one + 1])
                ins.then_inc(mix_dve, 1)
                dve.wait_ge(mix_dve, N * b + 1)
                for j in range(CH):
                    ins = dve.scalar_tensor_tensor(sprime[:, j, :], bvm[:, j, :], mmean[:, j:j + 1], s_gain[:, j, :],
                                                   ALU.mult, ALU.add)
                ins.then_inc(mix_dve, 1)
                dve.wait_ge(mix_pe, b + 1)
                m_ps = ps[:, 0:3, 0:C]
                dve.tensor_reduce(mmean[:, 0:3], m_ps, AX.X, ALU.add).then_inc(mix_dve, 1)
                dve.wait_ge(mix_dve, N * b + 3)
                for i in range(3):
                    ins = dve.scalar_tensor_tensor(m_cent[:, i, :], mmean[:, i:i + 1].broadcast_to([P, C]), -1.0 / C,
                                                   m_ps[:, i, :], ALU.mult, ALU.add)
                ins.then_inc(mix_dve, 1)
                dve.wait_ge(mix_dve, N * b + 4)
                dve.tensor_copy(m_hi[:, 0:2, :], m_cent[:, 0:2, :])
                dve.tensor_copy(m_hi[0:1, 2, :], m_cent[0:1, 2, :])
                dve.tensor_copy(s_gain[32:33, 0:1, 0:P].rearrange("p a d -> p (a d)").bitcast(F16),
                                m_cent[32:33, 2, :]).then_inc(mix_dve, 1)
                dve.wait_ge(mix_dve, N * b + 5)
                dve.tensor_tensor(m_lo[:], m_cent[:, 0:2, :], m_hi[:, 0:2, :], ALU.subtract)
                dve.tensor_tensor(m_hi[32:33, 2, :], m_cent[32:33, 2, :],
                                  s_gain[32:33, 0:1, 0:P].rearrange("p a d -> p (a d)").bitcast(F16),
                                  ALU.subtract).then_inc(mix_dve, 1)
                dve.wait_ge(mix_dve, N * b + 6)

            def with_positions(b, g, par):
                H = 2 * GROUPS * b + GROUPS + g
                if not (isinstance(g, int) and g < 2):
                    dve.wait_ge(lo_ready, H - 1)
                xg = x_group(b, g, par)
                row = bass.ds(g * GTILES, GTILES)
                add0 = posb[:, 0, row].unsqueeze(2).broadcast_to([P, GTILES, W])
                add1 = posb[:, 1, :].unsqueeze(1).broadcast_to([P, GTILES, W])
                for c, add in ((0, add0), (1, add1)):
                    ins = dve.scalar_tensor_tensor(u[par][:, c, :].rearrange("p (r w) -> p r w", w=W),
                                                   xg[:, c, :].rearrange("p (r w) -> p r w", w=W),
                                                   grstd[:, c:c + 1], add, ALU.mult, ALU.add)
                ins.then_inc(u_ready, 1)

            def out_stats(b, g, par):
                Gn = GROUPS * b + g
                dve.wait_ge(o_ready, Gn + 1)
                for t in range(GTILES):
                    ins = dve.bn_stats(obn[:, par, t, :], o_ps[par][:, t, :])
                ins.then_inc(obn_ready, 1)
                dve.wait_ge(obn_ready, Gn + 1)
                dve.tensor_tensor(otmp[:, par, 0, :], obn[:, par, :, 1], obn[:, par, :, 4], ALU.subtract)
                dve.tensor_tensor(otmp[:, par, 1, :], obn[:, par, :, 2], obn[:, par, :, 5], ALU.add).then_inc(ovar_step, 1)
                dve.wait_ge(ovar_step, 2 * Gn + 1)
                dve.scalar_tensor_tensor(otmp[:, par, 2, :], otmp[:, par, 0, :], C / 4.0, otmp[:, par, 0, :],
                                         ALU.mult, ALU.mult).then_inc(ovar_step, 1)
                dve.wait_ge(ovar_step, 2 * Gn + 2)
                dve.tensor_tensor(ovar[:, par, :], otmp[:, par, 1, :], otmp[:, par, 2, :], ALU.add).then_inc(ovar_ready, 1)

            def out_rstd(b, g, par):
                Gn = GROUPS * b + g
                dve.wait_ge(ostd_ready, Gn + 1)
                dve.reciprocal(orstd[:, par, :], ostd[:, par, :]).then_inc(orstd_ready, 1)

            def phase2_pair(b, it, more, first=False, last=False):
                for h in range(4):
                    g = 4 * it + h
                    if not (last and h == 3):
                        with_positions(b, g + 1, (h + 1) % 2)
                    out_stats(b, g, h % 2)
                    if more and not first and h % 2 == 0:
                        unit_stats(b + 1, 2 * it - 2 + h // 2, h // 2)
                    out_rstd(b, g, h % 2)

            def image(b, more):
                group_norm(b)
                normalise(b, 0, 0)
                group_shift(b)
                low_part(b, 0, 0)
                sweep(dve, phase1_group, b)
                inverse_std(b, PAIRS - 2, 2)
                sum_squares(b, PAIRS - 1, 3)
                inverse_std(b, PAIRS - 1, 3)
                mix(b)
                with_positions(b, 0, 0)
                phase2_pair(b, 0, more, first=True)
                with dve.Fori(1, UNITS // 2 - 1) as it:
                    phase2_pair(b, it, more)
                phase2_pair(b, UNITS // 2 - 1, more, last=True)
                if more:
                    unit_stats(b + 1, UNITS - 2, 0)
                    unit_stats(b + 1, UNITS - 1, 1)

            with dve.Fori(0, UNITS // 2) as k:
                unit_stats(0, 2 * k, 0)
                unit_stats(0, 2 * k + 1, 1)
            with dve.Fori(0, B - 1) as b:
                image(b, True)
            image(B - 1, False)

        @block.scalar
        def _(act):
            def high_part(b, phase, g, par):
                H = 2 * GROUPS * b + GROUPS * phase + g
                act.wait_ge(u_ready, H + 1)
                wait_parts_free(act, b, phase, g)
                act.copy(hi[par][:], u[par][:]).then_inc(hi_ready, 1)

            def square(b, p, q):
                Pn = PAIRS * b + p
                act.wait_ge(kv_evac, Pn + 1)
                if not (isinstance(p, int) and p < 2):
                    act.wait_ge(summed, Pn - 1)
                act.activation(sq[q % 2][:].rearrange("p (a c) -> p a c", c=C),
                               kv[q][:].rearrange("p t (a c) -> p (t a) c", a=2)[:, :, 0:C],
                               ACT.Square).then_inc(squared, 1)

            def kv_std(b, p, q):
                Pn = PAIRS * b + p
                act.wait_ge(summed, Pn + 1)
                act.activation(std[:, q, :], ssum[:, q, :], ACT.Sqrt, bias=eps[:, 1:2], scale=1.0 / DK).then_inc(std_ready, 1)

            def phase1_group(b, g, par):
                p, q = 2 * g, 2 * par
                first, last = ends(g)
                if not last:
                    high_part(b, 0, g + 1, 1 - par)
                square(b, p, q)
                if not first:
                    kv_std(b, p - 1, (q + 3) % 4)
                square(b, p + 1, q + 1)
                kv_std(b, p, q)

            def normalise_out(b, g, par):
                Gn = GROUPS * b + g
                act.wait_ge(ovar_ready, Gn + 1)
                act.activation(ostd[:, par, :], ovar[:, par, :], ACT.Sqrt, bias=eps[:, 2:3], scale=1.0 / C).then_inc(ostd_ready, 1)
                act.wait_ge(orstd_ready, Gn + 1)
                if not (isinstance(g, int) and g < 2):
                    act.wait_ge(t_ready, Gn - 1)
                for t in range(GTILES):
                    ins = act.activation(z[par][:, t, :], o_ps[par][:, t, :], ACT.Copy, scale=orstd[:, par, t:t + 1])
                ins.then_inc(z_ready, 1)

            def gain_bias(b, g, par):
                Gn = GROUPS * b + g
                act.wait_ge(t_ready, Gn + 1)
                if not (isinstance(g, int) and g < 2):
                    act.wait_ge(y_ready, Gn - 1)
                for c in range(CH):
                    ins = act.activation(wout[par][:, c, :], t_ps[par][:, c, :], ACT.Identity,
                                         bias=cols[:, 4, c:c + 1], scale=cols[:, 3, c:c + 1])
                ins.then_inc(w_ready, 1)

            def phase2_group(b, g, par):
                first, last = ends(g)
                if not last:
                    high_part(b, 1, g + 1, 1 - par)
                normalise_out(b, g, par)
                if not first:
                    gain_bias(b, g - 1, 1 - par)

            with act.Fori(0, B) as b:
                act.wait_ge(gn_pe, 2 * b + 2)
                act.activation(gstd[:], ps[:, 0, 2:2 + CH], ACT.Sqrt, bias=eps[:, 0:1]).then_inc(gn_act, 1)
                high_part(b, 0, 0, 0)
                sweep(act, phase1_group, b)
                kv_std(b, PAIRS - 1, 3)
                high_part(b, 1, 0, 0)
                sweep(act, phase2_group, b)
                gain_bias(b, GROUPS - 1, 1)

        @block.gpsimd
        def _(pool):
            pool.wait_ge(max_ready, 1)
            pool.partition_all_reduce(max_all[:], max_in[:], P, bass.bass_isa.ReduceOp.max).then_inc(setup_pool, 1)

            def scale_pair(b, p, q):
                Pn = PAIRS * b + p
                pool.wait_ge(rstd_ready, Pn + 1)
                if not (isinstance(p, int) and p < 2):
                    pool.wait_ge(scored, Pn - 1)
                r = rstd[:, q, :].rearrange("p (t a h) -> p t a h", t=2, a=2)
                pool.tensor_tensor(kaug[q % 2][:].rearrange("p t (h d) -> p t h d", d=DK)[:, :, :, 0:DK - 1],
                                   kv[q][:, :, 0:C].rearrange("p t (h d) -> p t h d", d=DK)[:, :, :, 0:DK - 1],
                                   r[:, :, 0, :].unsqueeze(3).broadcast_to([P, 2, HEADS, DK - 1]), ALU.mult
                                   ).then_inc(k_scaled, 1)
                v = kv[q][:, :, C + 1:2 * C + 1].rearrange("p t (h d) -> p t h d", d=DK)
                pool.tensor_tensor(v, v, r[:, :, 1, :].unsqueeze(3).broadcast_to([P, 2, HEADS, DK]), ALU.mult
                                   ).then_inc(k_scaled, 1)

            def low_part(b, g, par):
                H = 2 * GROUPS * b + GROUPS + g
                pool.wait_ge(hi_ready, H + 1)
                wait_parts_free(pool, b, 1, g)
                pool.tensor_tensor(lo[par][:], u[par][:], hi[par][:], ALU.subtract).then_inc(lo_ready, 1)

            def residual(b, g, par):
                Gn = GROUPS * b + g
                pool.wait_ge(w_ready, Gn + 1)
                xg = x_group(b, g, par)
                pool.tensor_tensor(xg, xg, wout[par], ALU.add).then_inc(y_ready, 1)

            def phase2_group(b, g, par):
                first, last = ends(g)
                if not last:
                    low_part(b, g + 1, 1 - par)
                if not first:
                    residual(b, g - 1, 1 - par)

            def ones_beside_v():
                one = kaug[0][:, 0, DK - 1:DK].unsqueeze(1).broadcast_to([P, 4, 1])
                for i in range(2):
                    ins = pool.tensor_tensor(kv[i][:].rearrange("p t (a c) -> p (t a) c", a=2)[:, :, C:C + 1],
                                             one, one, ALU.mult)
                ins.then_inc(kv_free, 1)

            with pool.Fori(0, B) as b:
                for q in range(4):
                    scale_pair(b, q, q)
                with pool.Fori(1, PAIRS // 4) as i:
                    for q in range(4):
                        scale_pair(b, 4 * i + q, q)
                low_part(b, 0, 0)
                sweep(pool, phase2_group, b)
                residual(b, GROUPS - 1, 1)
                pool.wait_ge(y_ready, GROUPS * b + GROUPS)
                ones_beside_v()

        @block.tensor
        def _(pe):
            pe.wait_ge(params_loaded, 16 * 13)
            for c in range(CH):
                for i, w in enumerate((wk_in, wv_in)):
                    for j in range(CH):
                        mm = pe.transpose(ps[:, c, i * C + j * P:i * C + (j + 1) * P], w[:, j, c * P:(c + 1) * P], ident)
            mm.then_inc(setup_pe, 1)
            pe.wait_ge(wc_ready, 1)
            pe.matmul(ps[:, 2, 0:C], pos[:, 1, :], wc[:, 1, 0:C], start=True, stop=True)
            for h in range(2):
                for d in range(2):
                    mm = pe.matmul(ps[d * HALF:(d + 1) * HALF, 3 + h, 0:C], pos[:, 0, h * HALF:(h + 1) * HALF],
                                   wc[:, 0, 0:C], start=True, stop=True)
            mm.then_inc(setup_pe, 1)
            pe.wait_ge(lmat_ready, 1)
            for j in range(CH):
                pe.matmul(ps[:, 5 + j, 0:C], lmat[:, j, :], wq_in[:, j, :], start=True, stop=True)
                mm = pe.matmul(ps[:, 5 + j, C:C + P], lmat[:, j, :], bq_rep[:, j, :], start=True, stop=True)
            mm.then_inc(setup_pe, 1)

            def project(b, g, t, par, out):
                px = slice(t * W, (t + 1) * W)
                row = g * GTILES + t
                if isinstance(g, int):
                    s = sel[:, row % HALF:row % HALF + 1]
                    r = rowpart[:, row // HALF, :]
                else:
                    s = sel[:, bass.ds(row % HALF, 1)]
                    r = rowpart[:, bass.ds(row // HALF, 1), :].rearrange("p a c -> p (a c)")
                pe.matmul(out, hi[par][:, 0, px], wkv_hi[:, 0, :], start=True, stop=False)
                pe.matmul(out, hi[par][:, 0, px], wkv_lo[:, 0, :], start=False, stop=False)
                pe.matmul(out[:, 0:C], s.broadcast_to([P, P]), r, start=False, stop=False, skip_group_check=True)
                pe.matmul(out, lo[par][:, 0, px], wkv_hi[:, 0, :], start=False, stop=False)
                pe.matmul(out, hi[par][:, 1, px], wkv_hi[:, 1, :], start=False, stop=False)
                pe.matmul(out, hi[par][:, 1, px], wkv_lo[:, 1, :], start=False, stop=False)
                return pe.matmul(out, lo[par][:, 1, px], wkv_hi[:, 1, :], start=False, stop=True)

            def project_pair(b, g, h, par):
                Pn = PAIRS * b + 2 * g + h
                H = 2 * GROUPS * b + g
                if h == 0:
                    pe.wait_ge(lo_ready, H + 1)
                if not (isinstance(g, int) and g == 0):
                    pe.wait_ge(kv_evac, Pn - 1)
                for t in range(2):
                    mm = project(b, g, 2 * h + t, par, kv_ps[h][:, t, :])
                mm.then_inc(kv_proj, 1)

            def scores(b, p, q):
                Pn = PAIRS * b + p
                pe.wait_ge(k_scaled, 2 * Pn + 2)
                for t in range(2):
                    for j in range(CH):
                        v0 = C + j * (P + 1)
                        mm = pe.matmul(s_ps[j], kaug[q % 2][:, t, j * P:(j + 1) * P], kv[q][:, t, v0:v0 + P + 1],
                                       start=False, stop=False, skip_group_check=True)
                mm.then_inc(scored, 1)

            def phase1_group(b, g, par):
                q = 2 * par
                score = not (isinstance(g, int) and g < 2)
                if score:
                    scores(b, 2 * g - 4, q)
                project_pair(b, g, 0, par)
                if score:
                    scores(b, 2 * g - 3, q + 1)
                project_pair(b, g, 1, par)
                if isinstance(g, int) and g == 1:
                    pe.wait_ge(kv_free, b + 1)
                    for j in range(CH):
                        pe.matmul(s_ps[j], zero16[:, 0:P], zero16[:], start=True, stop=False, skip_group_check=True)

            def project_out(b, g, par):
                H = 2 * GROUPS * b + GROUPS + g
                Gn = GROUPS * b + g
                pe.wait_ge(lo_ready, H + 1)
                if not (isinstance(g, int) and g < 2):
                    pe.wait_ge(z_ready, Gn - 1)
                for t in range(GTILES):
                    px = slice(t * W, (t + 1) * W)
                    out = o_ps[par][:, t, :]
                    first = True
                    for c in range(CH):
                        for st, m in ((hi, m_hi), (hi, m_lo), (lo, m_hi)):
                            pe.matmul(out, st[par][:, c, px], m[:, c, :], start=first, stop=False)
                            first = False
                    mm = pe.matmul(out, ones_hl[:], m_hi[:, 2, :], start=False, stop=True)
                mm.then_inc(o_ready, 1)
                return mm

            def transpose_back(b, g, par):
                Gn = GROUPS * b + g
                pe.wait_ge(z_ready, Gn + 1)
                if not (isinstance(g, int) and g < 2):
                    pe.wait_ge(w_ready, Gn - 1)
                for t in range(GTILES):
                    for c in range(CH):
                        mm = pe.transpose(t_ps[par][:, c, t * W:(t + 1) * W], z[par][:, t, c * P:(c + 1) * P], ident)
                mm.then_inc(t_ready, 1)

            def phase2_group(b, g, par):
                first, last = ends(g)
                project_out(b, g, par)
                if not first:
                    transpose_back(b, g - 1, 1 - par)

            with pe.Fori(0, B) as b:
                pe.wait_ge(gn_dve, 8 * b + 1)
                pe.matmul(ps[:, 0, 0:CH], const("blk8"), mv[:, :, 0], start=True, stop=True).then_inc(gn_pe, 1)
                pe.wait_ge(gn_dve, 8 * b + 5)
                pe.matmul(ps[:, 0, 2:2 + CH], const("blk8"), gvar[:], start=True, stop=True).then_inc(gn_pe, 1)
                sweep(pe, phase1_group, b)
                for p in range(PAIRS - 4, PAIRS):
                    scores(b, p, p % 4)
                for j in range(CH):
                    mm = pe.matmul(s_ps[j], zero16[:, 0:P], zero16[:], start=False, stop=True, skip_group_check=True)
                mm.then_inc(sums_done, 1)
                pe.wait_ge(mix_dve, 6 * b + 2)
                for m in range(3):
                    for j in range(CH):
                        st = wql[:, j, m * P:(m + 1) * P] if m < 2 else bql[:, j, :]
                        mm = pe.matmul(ps[:, m, j * P:(j + 1) * P], st, sprime[:, j, :], start=True, stop=True)
                mm.then_inc(mix_pe, 1)
                pe.wait_ge(mix_dve, 6 * b + 6)
                sweep(pe, phase2_group, b)
                transpose_back(b, GROUPS - 1, 1)


def _constants():
    import numpy as np
    f = np.float32
    out = np.zeros((P, NCONST), f)

    def put(name, a):
        out[:, CAT[name][0]:CAT[name][1]] = a
    put("ident", np.eye(P, dtype=f))
    same = np.kron(np.eye(P // DK, dtype=f), np.ones((DK, DK), f))
    put("mask", same)
    put("blk8", np.kron(np.eye(P // 8, dtype=f), np.full((8, 8), 0.125, f)))
    rot = np.eye(DK, dtype=f)
    rot[DK - 1, :] = -1
    rot[:, DK - 1] = 0
    one = np.zeros((DK, DK), f)
    one[:, DK - 1] = 1
    put("lrot", np.kron(np.eye(P // DK, dtype=f), rot))
    put("lone", np.kron(np.eye(P // DK, dtype=f), one))
    half = C // 2
    t = (np.arange(1, W + 1, dtype=f) / f(W + 1e-6) * f(2.0 * np.pi)).astype(f)
    dim = np.arange(half, dtype=f)
    dim = (f(10000.0) ** (f(2.0) * np.floor(dim / f(2.0)) / f(half))).astype(f)
    a = (t[None, :] / dim[:, None]).astype(f)
    feat = np.where(np.arange(half)[:, None] % 2 == 0, np.sin(a), np.cos(a)).astype(f)
    put("pos", np.concatenate([feat, feat], axis=1))
    p = np.arange(P)
    put("sel", (p[:, None] % HALF == np.arange(HALF)[None, :]).astype(f))
    put("ones", np.repeat(((p == 0) | (p == 32)).astype(f)[:, None], P, axis=1))
    return out


_INS = ["x", "L0_conv_Wq", "L0_conv_bq", "L0_conv_Wk", "L0_conv_bk", "L0_conv_Wv", "L0_conv_bv", "L0_conv_gK",
        "L0_conv_bK", "L0_conv_gV", "L0_conv_bV", "L0_conv_g_ln", "L0_conv_b_ln"]


def kernel(**inputs):
    import numpy as _np
    import concourse.bacc as _bacc
    from concourse import mybir as _mybir
    from concourse.bass_utils import run_bass_kernel_spmd as _run

    nc = _bacc.Bacc("TRN2", target_bir_lowering=False, num_devices=1)
    arrays, args = {}, []
    for name in _INS:
        a = _np.ascontiguousarray(inputs[name])
        arrays[f"in_{name}_dram"] = a
        args.append(nc.dram_tensor(f"in_{name}_dram", a.shape, _mybir.dt.from_np(a.dtype), kind="ExternalInput").ap())
    arrays["consts_dram"] = _constants()
    args.append(nc.dram_tensor("consts_dram", (P, NCONST), _mybir.dt.float32, kind="ExternalInput").ap())
    args.append(nc.dram_tensor("out_0_dram", (B, C, ROWS, W), _mybir.dt.float32, kind="ExternalOutput").ap())
    build(nc, *args)
    r = _run(nc, [arrays], core_ids=[0])
    return r.results[0]["out_0_dram"]
```

```python
from contextlib import ExitStack

import concourse.bass as bass
from concourse import mybir

ALU = mybir.AluOpType
ACT = mybir.ActivationFunctionType
F32 = mybir.dt.float32
F16 = mybir.dt.float16
AX = mybir.AxisListType

P = 128
B = 8
C = 256
CH = C // P
W = 128
ROWS = 128
NPIX = ROWS * W
HEADS = 8
DK = C // HEADS
HPC = HEADS // CH
GTILES = 4
GPIX = GTILES * W
GROUPS = ROWS // GTILES
PAIRS = 2 * GROUPS
UNIT = 2 * GPIX
UNITS = NPIX // UNIT
SPARE = 2
SLOTS = UNITS + SPARE
NUNITS = B * UNITS
HALF = ROWS // 2
EPS = 1e-5
KVR = 4
VROW = C + 1 + C + 1
WBOUND = 64.0
MBOUND = 32768.0

CONSTS = [("ident", P), ("blk8", P), ("pos", 2 * P), ("lrot", P), ("lone", P), ("mask", P), ("sel", HALF), ("ones", P)]
CAT = {}
_at = 0
for _name, _n in CONSTS:
    CAT[_name] = (_at, _at + _n)
    _at += _n
NCONST = _at
NKEPT = CAT["pos"][1]


def sweep(eng, body, b, head=2):
    for g in range(head):
        body(b, g, g % 2)
    with eng.Fori(head // 2, GROUPS // 2 - 1) as i:
        body(b, 2 * i, 0)
        body(b, 2 * i + 1, 1)
    for g in (GROUPS - 2, GROUPS - 1):
        body(b, g, g % 2)


def ends(g):
    return (isinstance(g, int) and g == 0, isinstance(g, int) and g == GROUPS - 1)


def build(nc, x, Wq, bq, Wk, bk, Wv, bv, gK, bK, gV, bV, g_ln, b_ln, consts, y):
    with ExitStack() as ctx:
        def sb(name, shape, dt=F32):
            return ctx.enter_context(nc.sbuf_tensor(name, shape, dt))

        def sem(name):
            return ctx.enter_context(nc.semaphore(name))

        xr = sb("x_ring", [P, SLOTS, CH, UNIT])
        wkv_hi = sb("wkv_hi", [P, CH, 2 * C], F16)
        wkv_lo = sb("wkv_lo", [P, CH, 2 * C], F16)
        rowpart = sb("rowpart", [P, 2, C], F16)
        sel = sb("sel", [P, HALF], F16)
        ones_hl = sb("ones_hl", [P, P], F16)
        kv_add = sb("kv_add", [P, 2 * C])
        cst = sb("cst", [P, NKEPT])
        posb = sb("posb", [P, CH, P])
        wql = sb("wql", [P, CH, C])
        bql = sb("bql", [P, CH, P])
        gvm = sb("gvm", [P, CH, P])
        bvm = sb("bvm", [P, CH, P])
        cols = sb("cols", [P, 5, CH])
        sprime = sb("sprime", [P, CH, P])
        m_hi = sb("m_hi", [P, 3, C], F16)
        m_lo = sb("m_lo", [P, 2, C], F16)
        u = [sb(f"u{i}", [P, CH, GPIX]) for i in range(2)]
        hi = [sb(f"hi{i}", [P, CH, GPIX], F16) for i in range(2)]
        lo = [sb(f"lo{i}", [P, CH, GPIX], F16) for i in range(2)]
        kv = [sb(f"kv{i}", [P, 2, VROW]) for i in range(KVR)]
        sq = [sb(f"sq{i}", [P, 2 * 2 * C]) for i in range(2)]
        ssum = sb("ssum", [P, 4, 2 * 2 * HEADS])
        std = sb("std", [P, 4, 2 * 2 * HEADS])
        rstd = sb("rstd", [P, 4, 2 * 2 * HEADS])
        stats = sb("stats", [P, CH, GROUPS, 6])
        obn = sb("obn", [P, 2, GTILES, 6])
        otmp = sb("otmp", [P, 2, 3, GTILES])
        ovar = sb("ovar", [P, 2, GTILES])
        ostd = sb("ostd", [P, 2, GTILES])
        orstd = sb("orstd", [P, 2, GTILES])
        mv = sb("mv", [P, CH, 2])
        gmean = sb("gmean", [P, CH])
        gdev = sb("gdev", [P, CH])
        gsq = sb("gsq", [P, CH])
        gvar = sb("gvar", [P, CH])
        gstd = sb("gstd", [P, CH])
        grstd = sb("grstd", [P, CH])
        gshift = sb("gshift", [P, CH])
        eps = sb("eps", [P, 4])
        small = sb("small", [P, 32])
        max_in = sb("max_in", [P, 8])
        max_all = sb("max_all", [P, 8])
        zero16 = sb("zero16", [P, P + 1], F16)
        mmean = sb("mmean", [P, 4])
        z = [s[:].rearrange("p (t c) -> p t c", t=GTILES) for s in sq]
        wout = [t[:].rearrange("p a b -> p (a b)")[:, 0:CH * GPIX].rearrange("p (c t) -> p c t", c=CH) for t in kv[0:2]]
        TEMP_SLOT = SLOTS - 6
        flat = xr[:].rearrange("p s c t -> p (s c t)")[:, TEMP_SLOT * CH * UNIT:]

        def temp(i, n):
            return flat[:, i * 1024:i * 1024 + n]
        wk_in = temp(0, 2 * C).rearrange("p (j c) -> p j c", j=CH)
        wv_in = temp(1, 2 * C).rearrange("p (j c) -> p j c", j=CH)
        wq_in = temp(2, 2 * C).rearrange("p (j c) -> p j c", j=CH)
        bias_in = temp(3, 2 * C)
        gv_in = temp(4, 2 * C)
        wt = temp(5, 1024).rearrange("p (c d) -> p c d", c=CH)
        wc = temp(6, 1024).rearrange("p (c d) -> p c d", c=CH)
        lmat = temp(7, CH * P).rearrange("p (j d) -> p j d", j=CH)
        lone_g = temp(8, CH * P).rearrange("p (j d) -> p j d", j=CH)
        bias_c = temp(9, 2 * C)
        bq_rep = temp(10, CH * P).rearrange("p (j d) -> p j d", j=CH)
        cst_setup = temp(11, NCONST - NKEPT)
        m_cent = sq[0][:, 0:3 * C].rearrange("p (m c) -> p m c", m=3)
        s_gain = sq[1][:, 0:CH * P].rearrange("p (j d) -> p j d", j=CH)
        bias_hi = sq[1][:, CH * P:CH * P + P].bitcast(F16)

        ps = ctx.enter_context(nc.psum_tensor("ps", [P, 8, 512], F32))
        kv_ps = [ps[:, 2 * i:2 * i + 2, :] for i in range(2)]
        o_ps = [ps[:, 2 * i:2 * i + 2, :].rearrange("p a (t c) -> p (a t) c", t=2) for i in range(2)]
        s_ps = [ps[:, 4 + j, 0:P + 1] for j in range(CH)]
        t_ps = [ps[:, 4 + 2 * i:6 + 2 * i, :] for i in range(2)]

        def const(name):
            a, b_ = CAT[name]
            return cst[:, a:b_] if b_ <= NKEPT else cst_setup[:, a - NKEPT:b_ - NKEPT]
        ident = const("ident")
        pos = const("pos").rearrange("p (c t) -> p c t", c=CH)

        params_loaded = sem("params_loaded")
        loaded = [sem(f"loaded{i}") for i in range(2)]
        stored = [sem(f"stored{i}") for i in range(2)]
        setup_dve = sem("setup_dve")
        setup_pe = sem("setup_pe")
        setup_pool = sem("setup_pool")
        max_ready = sem("max_ready")
        wc_ready = sem("wc_ready")
        lmat_ready = sem("lmat_ready")
        ring_free = sem("ring_free")
        stats_done = sem("stats_done")
        gn_dve = sem("gn_dve")
        gn_pe = sem("gn_pe")
        gn_act = sem("gn_act")
        u_ready = sem("u_ready")
        hi_ready = sem("hi_ready")
        lo_ready = sem("lo_ready")
        kv_proj = sem("kv_proj")
        kv_evac = sem("kv_evac")
        squared = sem("squared")
        k_ones = sem("k_ones")
        summed = sem("summed")
        std_ready = sem("std_ready")
        rstd_ready = sem("rstd_ready")
        k_scaled = sem("k_scaled")
        scored = sem("scored")
        sums_done = sem("sums_done")
        kv_free = sem("kv_free")
        mix_dve = sem("mix_dve")
        mix_pe = sem("mix_pe")
        o_ready = sem("o_ready")
        obn_ready = sem("obn_ready")
        ovar_step = sem("ovar_step")
        ovar_ready = sem("ovar_ready")
        ostd_ready = sem("ostd_ready")
        orstd_ready = sem("orstd_ready")
        z_ready = sem("z_ready")
        t_ready = sem("t_ready")
        w_ready = sem("w_ready")
        y_ready = sem("y_ready")

        x_dram = x.rearrange("b (c p) (k r) w -> b k p c (r w)", p=P, k=UNITS)
        y_dram = y.rearrange("b (c p) (k r) w -> b k p c (r w)", p=P, k=UNITS)

        def slot(n):
            return n % SLOTS

        def x_group(b, g, parity):
            s = slot(UNITS * b + (g - parity) // 2)
            t = slice(parity * GPIX, (parity + 1) * GPIX)
            if isinstance(s, int):
                return xr[:, s, :, t]
            return xr[:, bass.ds(s, 1), :, t].rearrange("p a c t -> p (a c) t")

        def wait_parts_free(eng, b, phase, g):
            if phase == 0:
                if not (isinstance(g, int) and g < 2):
                    eng.wait_ge(kv_proj, PAIRS * b + 2 * g - 2)
            elif isinstance(g, int) and g < 2:
                eng.wait_ge(kv_proj, PAIRS * b + PAIRS)
            else:
                eng.wait_ge(o_ready, GROUPS * b + g - 1)

        block = ctx.enter_context(nc.Block())

        @block.sync
        def _(sp):
            def load(n, par):
                if not isinstance(n, int) or n >= 2:
                    sp.wait_ge(loaded[par], (n - par) // 2 * 16)
                s = slot(n)
                if isinstance(n, int):
                    sp.dma_start(xr[:, s, :, :], x_dram[n // UNITS, n % UNITS]).then_inc(loaded[par], 16)
                else:
                    sp.dma_start(xr[:, bass.ds(s, 1), :, :].rearrange("p a c t -> p (a c) t"),
                                 x_dram[bass.ds(n // UNITS, 1), bass.ds(n % UNITS, 1)].rearrange("a k p c t -> p (a k c) t")
                                 ).then_inc(loaded[par], 16)

            def store(m, par):
                sp.wait_ge(y_ready, 2 * m + 2)
                s = slot(m)
                if isinstance(m, int):
                    sp.dma_start(y_dram[m // UNITS, m % UNITS], xr[:, s, :, :]).then_inc(stored[par], 16)
                else:
                    sp.dma_start(y_dram[bass.ds(m // UNITS, 1), bass.ds(m % UNITS, 1)].rearrange("a k p c t -> p (a k c) t"),
                                 xr[:, bass.ds(s, 1), :, :].rearrange("p a c t -> p (a c) t")
                                 ).then_inc(stored[par], 16)

            def store_and_refill(m, par):
                store(m, par)
                sp.wait_ge(stored[par], ((m - par) // 2 + 1) * 16)
                load(m + SLOTS, (par + SLOTS) % 2)

            sp.dma_start(cst[:], consts[:, 0:NKEPT]).then_inc(params_loaded, 16)
            sp.dma_start(cst_setup, consts[:, NKEPT:NCONST]).then_inc(params_loaded, 16)
            for dst, src in ((wk_in, Wk), (wv_in, Wv), (wq_in, Wq)):
                sp.dma_start(dst, src.rearrange("(j p) c -> p j c", p=P)).then_inc(params_loaded, 16)
            for i, src in enumerate((bk, bv)):
                sp.dma_start(bias_in[:, i * C:(i + 1) * C], src.rearrange("(a c) -> a c", a=1).partition_broadcast(P)
                             ).then_inc(params_loaded, 16)
            for i, src in enumerate((gV, bV)):
                sp.dma_start(gv_in[:, i * C:(i + 1) * C],
                             src.rearrange("h d -> (h d)").rearrange("(a c) -> a c", a=1).partition_broadcast(P)
                             ).then_inc(params_loaded, 16)
            for i, src in enumerate((gK.rearrange("h d -> (h d)"), bK.rearrange("h d -> (h d)"), bq, g_ln, b_ln)):
                sp.dma_start(cols[:, i, :], src.rearrange("(j p) -> p j", p=P), allow_slow_non_contiguous=True
                             ).then_inc(params_loaded, 16)
            for n in range(SLOTS):
                if n == TEMP_SLOT:
                    sp.wait_ge(ring_free, 1)
                load(n, n % 2)
            refills = NUNITS - SLOTS
            with sp.Fori(0, refills // 2) as i:
                store_and_refill(2 * i, 0)
                store_and_refill(2 * i + 1, 1)
            for m in range(refills // 2 * 2, refills):
                store_and_refill(m, m % 2)
            for m in range(refills, NUNITS):
                store(m, m % 2)
            sp.wait_ge(stored[0], NUNITS // 2 * 16)
            sp.wait_ge(stored[1], NUNITS // 2 * 16)

        @block.vector
        def _(dve):
            step = [0]

            def link(ins):
                step[0] += 1
                ins.then_inc(setup_dve, 1)
                dve.wait_ge(setup_dve, step[0])
            dve.wait_ge(params_loaded, 16 * 14)
            dve.tensor_copy(sel[:], const("sel"))
            dve.tensor_copy(ones_hl[:], const("ones"))
            dve.memset(m_hi[:], 0.0)
            dve.memset(zero16[:], 0.0)
            for t in kv:
                ins = dve.memset(t[:], 1.0)
            ins.then_inc(kv_free, 1)
            dve.memset(eps[:, 0:3], EPS)
            dve.memset(eps[:, 3:4], 1.0)
            dve.wait_ge(setup_pe, 1)
            link(dve.tensor_copy(wt, ps[:, 0:CH, :]))
            wt_h = wt.rearrange("p c (h d) -> p c h d", d=DK)
            hm = small[:, 0:32].rearrange("p (c h) -> p c h", c=CH)
            link(dve.tensor_reduce(hm, wt_h, AX.X, ALU.add))
            link(dve.tensor_scalar(small[:, 0:32], small[:, 0:32], -1.0 / DK, None, ALU.mult))
            for c in range(CH):
                ins = dve.tensor_tensor(wc[:, c, :].rearrange("p (h d) -> p h d", d=DK), wt_h[:, c],
                                        hm[:, c, :].unsqueeze(2).broadcast_to([P, 16, DK]), ALU.add)
            link(ins)
            bias_h = bias_in.rearrange("p (h d) -> p h d", d=DK)
            link(dve.tensor_reduce(small[:, 0:16], bias_h, AX.X, ALU.add))
            link(dve.tensor_scalar(small[:, 0:16], small[:, 0:16], -1.0 / DK, None, ALU.mult))
            link(dve.tensor_tensor(bias_c.rearrange("p (h d) -> p h d", d=DK), bias_h,
                                   small[:, 0:16].unsqueeze(2).broadcast_to([P, 16, DK]), ALU.add))
            link(dve.memset(small[:], 0.0))

            def absmax(col, src):
                return dve.tensor_reduce(small[:, col:col + 1], src, AX.XY, ALU.max, apply_absolute_value=True)
            absmax(0, wc)
            absmax(1, wq_in)
            for col, src in ((2, cols[:, 0:1, :]), (3, cols[:, 1:2, :]), (6, cols[:, 2:3, :])):
                absmax(col, src)
            absmax(4, gv_in[:, 0:C].rearrange("p (a c) -> p a c", a=1))
            link(absmax(5, gv_in[:, C:2 * C].rearrange("p (a c) -> p a c", a=1)))
            link(dve.tensor_tensor(small[:, 1:2], small[:, 1:2], small[:, 6:7], ALU.max))
            dve.tensor_copy(max_in[:], small[:, 0:8]).then_inc(max_ready, 1)
            dve.wait_ge(setup_pool, 1)
            link(dve.tensor_scalar(small[:, 8:16], max_all[:], 1e-12, None, ALU.max))
            link(dve.scalar_tensor_tensor(small[:, 16:17], small[:, 10:11], float(DK) ** 0.5, small[:, 11:12], ALU.mult, ALU.add))
            link(dve.scalar_tensor_tensor(small[:, 17:18], small[:, 12:13], float(DK) ** 0.5, small[:, 13:14], ALU.mult, ALU.add))
            link(dve.tensor_scalar(small[:, 16:18], small[:, 16:18], 1e-3, None, ALU.max))
            link(dve.tensor_tensor(small[:, 18:19], small[:, 16:17], small[:, 17:18], ALU.mult))
            link(dve.tensor_tensor(small[:, 19:20], small[:, 18:19], small[:, 9:10], ALU.mult))
            link(dve.reciprocal(small[:, 20:21], small[:, 8:9]))
            link(dve.reciprocal(small[:, 21:22], small[:, 19:20]))
            link(dve.tensor_scalar(small[:, 22:23], small[:, 20:21], WBOUND, None, ALU.mult))
            link(dve.tensor_scalar(small[:, 23:24], small[:, 21:22], MBOUND / (2 * DK), None, ALU.mult))
            link(dve.tensor_scalar(small[:, 24:25], small[:, 23:24], 1.0 / NPIX, None, ALU.mult))
            link(dve.tensor_scalar(eps[:, 1:2], small[:, 22:23], small[:, 22:23], EPS, ALU.mult, ALU.mult))
            link(dve.tensor_scalar(eps[:, 2:3], small[:, 23:24], small[:, 23:24], EPS / 4, ALU.mult, ALU.mult))
            link(dve.tensor_scalar(wc, wc, small[:, 22:23], None, ALU.mult))
            link(dve.tensor_scalar(bias_c, bias_c, small[:, 22:23], None, ALU.mult))
            dve.tensor_copy(wkv_hi[:], wc).then_inc(wc_ready, 1)
            dve.wait_ge(wc_ready, 1)
            link(dve.tensor_tensor(wkv_lo[:], wc, wkv_hi[:], ALU.subtract))
            for j in range(CH):
                ins = dve.tensor_scalar(lone_g[:, j, :], const("lone"), cols[:, 1, j:j + 1], None, ALU.mult)
            link(ins)
            for j in range(CH):
                dve.scalar_tensor_tensor(lmat[:, j, :], const("lrot"), cols[:, 0, j:j + 1], lone_g[:, j, :], ALU.mult, ALU.add)
            for j in range(CH):
                dve.tensor_copy(bq_rep[:, j, :], cols[:, 2, j:j + 1].broadcast_to([P, P]))
                for t, o in ((gvm, 0), (bvm, C)):
                    ins = dve.tensor_tensor(t[:, j, :], gv_in[:, o + j * P:o + (j + 1) * P], const("mask"), ALU.mult)
            ins.then_inc(lmat_ready, 1)
            dve.wait_ge(setup_pe, 2)
            dve.tensor_tensor(kv_add[:, 0:C], ps[:, 2, 0:C], bias_c[:, 0:C], ALU.add)
            dve.tensor_copy(kv_add[:, C:2 * C], bias_c[:, C:2 * C])
            for h in range(2):
                dve.tensor_copy(rowpart[0:HALF, h, :], ps[0:HALF, 3 + h, 0:C])
                link(dve.tensor_copy(sq[0][HALF:P, h * C:h * C + C // 2].bitcast(F16), ps[HALF:P, 3 + h, 0:C]))
                link(dve.tensor_tensor(rowpart[HALF:P, h, :], ps[HALF:P, 3 + h, 0:C],
                                       sq[0][HALF:P, h * C:h * C + C // 2].bitcast(F16), ALU.subtract))
            dve.wait_ge(setup_pe, 3)
            for j in range(CH):
                dve.tensor_scalar(wql[:, j, :], ps[:, 5 + j, 0:C], small[:, 24:25], None, ALU.mult)
                ins = dve.tensor_scalar(bql[:, j, :], ps[:, 5 + j, C:C + P], small[:, 24:25], None, ALU.mult)
            link(ins)
            dve.drain().then_inc(ring_free, 1)

            def unit_stats(b, k, par, parts=((0, 0), (0, 1), (1, 0), (1, 1))):
                n = UNITS * b + k
                dve.wait_ge(loaded[par], (n - par) // 2 * 16 + 16)
                for h, c in parts:
                    xg = x_group(b, 2 * k + h, h)
                    if isinstance(k, int):
                        dst = stats[:, c, 2 * k + h, :]
                    else:
                        dst = stats[:, c, bass.ds(2 * k + h, 1), :].rearrange("p a s -> p (a s)")
                    dve.bn_stats(dst, xg[:, c, :]).then_inc(stats_done, 1)

            def group_norm(b):
                G = 8
                dve.wait_ge(stats_done, 4 * UNITS * b + 4 * UNITS)
                dve.memset(mmean[:, 3:4], 0.0)
                for c in range(CH):
                    ins = dve.bn_aggr(mv[:, c, :], stats[:, c].rearrange("p g s -> p (g s)"))
                ins.then_inc(gn_dve, 1)
                dve.wait_ge(gn_pe, 2 * b + 1)
                dve.tensor_copy(gmean[:], ps[:, 0, 0:CH]).then_inc(gn_dve, 1)
                dve.wait_ge(gn_dve, G * b + 2)
                dve.tensor_tensor(gdev[:], mv[:, :, 0], gmean[:], ALU.subtract).then_inc(gn_dve, 1)
                dve.wait_ge(gn_dve, G * b + 3)
                dve.tensor_tensor(gsq[:], gdev[:], gdev[:], ALU.mult).then_inc(gn_dve, 1)
                dve.wait_ge(gn_dve, G * b + 4)
                dve.tensor_tensor(gvar[:], gsq[:], mv[:, :, 1], ALU.add).then_inc(gn_dve, 1)
                dve.wait_ge(gn_act, b + 1)
                dve.reciprocal(grstd[:], gstd[:]).then_inc(gn_dve, 1)
                dve.wait_ge(gn_dve, G * b + 6)

            def group_shift(b):
                G = 8
                dve.scalar_tensor_tensor(gshift[:], gmean[:], -1.0, grstd[:], ALU.mult, ALU.mult).then_inc(gn_dve, 1)
                dve.wait_ge(kv_free, b + 1)
                dve.wait_ge(gn_dve, G * b + 7)
                for c in range(CH):
                    ins = dve.tensor_scalar(posb[:, c, :], pos[:, c, :], gshift[:, c:c + 1], None, ALU.add)
                ins.then_inc(gn_dve, 1)
                dve.wait_ge(gn_dve, G * b + 8)

            def normalise(b, g, par):
                H = 2 * GROUPS * b + g
                if not (isinstance(g, int) and g < 2):
                    dve.wait_ge(hi_ready, H - 1)
                xg = x_group(b, g, par)
                for c in range(CH):
                    ins = dve.tensor_scalar(u[par][:, c, :], xg[:, c, :], gmean[:, c:c + 1], grstd[:, c:c + 1],
                                            ALU.subtract, ALU.mult)
                ins.then_inc(u_ready, 1)

            def low_part(b, phase, g, par):
                H = 2 * GROUPS * b + GROUPS * phase + g
                dve.wait_ge(hi_ready, H + 1)
                wait_parts_free(dve, b, phase, g)
                dve.tensor_tensor(lo[par][:], u[par][:], hi[par][:], ALU.subtract).then_inc(lo_ready, 1)

            def evacuate(b, p, q):
                Pn = PAIRS * b + p
                dve.wait_ge(kv_proj, Pn + 1)
                if not (isinstance(p, int) and p < KVR):
                    dve.wait_ge(scored, Pn - KVR + 1)
                dst = kv[q][:].rearrange("p t (a c) -> p t a c", a=2)[:, :, :, 0:C]
                src = kv_ps[q % 2].rearrange("p t (a c) -> p t a c", a=2)
                add = kv_add[:].rearrange("p (a c) -> p a c", a=2).unsqueeze(1).broadcast_to([P, 2, 2, C])
                dve.tensor_tensor(dst, src, add, ALU.add).then_inc(kv_evac, 1)

            def sum_squares(b, p, q):
                Pn = PAIRS * b + p
                dve.wait_ge(squared, Pn + 1)
                dve.tensor_reduce(ssum[:, q, :], sq[q % 2][:].rearrange("p (h d) -> p h d", d=DK),
                                  AX.X, ALU.add).then_inc(summed, 1)

            def inverse_std(b, p, q):
                Pn = PAIRS * b + p
                dve.wait_ge(std_ready, Pn + 1)
                dve.reciprocal(rstd[:, q, :], std[:, q, :]).then_inc(rstd_ready, 1)

            def phase1_group(b, g, par):
                p, q = 2 * g, 2 * par
                first, last = ends(g)
                if not last:
                    normalise(b, g + 1, 1 - par)
                evacuate(b, p, q)
                if not first:
                    inverse_std(b, p - 2, (q + 2) % 4)
                if not last:
                    low_part(b, 0, g + 1, 1 - par)
                if not first:
                    sum_squares(b, p - 1, (q + 3) % 4)
                evacuate(b, p + 1, q + 1)
                if not first:
                    inverse_std(b, p - 1, (q + 3) % 4)
                sum_squares(b, p, q)

            def mix(b):
                N = 6
                dve.wait_ge(sums_done, b + 1)
                for j in range(CH):
                    v0, one = (1, 0) if j == 0 else (0, P)
                    dve.tensor_tensor(s_gain[:, j, :], s_ps[j][:, v0:v0 + P], gvm[:, j, :], ALU.mult)
                    ins = dve.tensor_copy(mmean[:, j:j + 1], s_ps[j][:, one:one + 1])
                ins.then_inc(mix_dve, 1)
                dve.wait_ge(mix_dve, N * b + 1)
                for j in range(CH):
                    ins = dve.scalar_tensor_tensor(sprime[:, j, :], bvm[:, j, :], mmean[:, j:j + 1], s_gain[:, j, :],
                                                   ALU.mult, ALU.add)
                ins.then_inc(mix_dve, 1)
                dve.wait_ge(mix_pe, b + 1)
                m_ps = ps[:, 0:3, 0:C]
                dve.tensor_reduce(mmean[:, 0:3], m_ps, AX.X, ALU.add).then_inc(mix_dve, 1)
                dve.wait_ge(mix_dve, N * b + 3)
                for i in range(3):
                    ins = dve.scalar_tensor_tensor(m_cent[:, i, :], mmean[:, i:i + 1].broadcast_to([P, C]), -1.0 / C,
                                                   m_ps[:, i, :], ALU.mult, ALU.add)
                ins.then_inc(mix_dve, 1)
                dve.wait_ge(mix_dve, N * b + 4)
                dve.tensor_copy(m_hi[:, 0:2, :], m_cent[:, 0:2, :])
                dve.tensor_copy(m_hi[0:1, 2, :], m_cent[0:1, 2, :])
                dve.tensor_copy(bias_hi[32:33, :],
                                m_cent[32:33, 2, :]).then_inc(mix_dve, 1)
                dve.wait_ge(mix_dve, N * b + 5)
                dve.tensor_tensor(m_lo[:], m_cent[:, 0:2, :], m_hi[:, 0:2, :], ALU.subtract)
                dve.tensor_tensor(m_hi[32:33, 2, :], m_cent[32:33, 2, :],
                                  bias_hi[32:33, :],
                                  ALU.subtract).then_inc(mix_dve, 1)
                dve.wait_ge(mix_dve, N * b + 6)

            def with_positions(b, g, par):
                H = 2 * GROUPS * b + GROUPS + g
                dve.wait_ge(lo_ready, H - 1)
                xg = x_group(b, g, par)
                row = bass.ds(g * GTILES, GTILES)
                add0 = posb[:, 0, row].unsqueeze(2).broadcast_to([P, GTILES, W])
                add1 = posb[:, 1, :].unsqueeze(1).broadcast_to([P, GTILES, W])
                for c, add in ((0, add0), (1, add1)):
                    ins = dve.scalar_tensor_tensor(u[par][:, c, :].rearrange("p (r w) -> p r w", w=W),
                                                   xg[:, c, :].rearrange("p (r w) -> p r w", w=W),
                                                   grstd[:, c:c + 1], add, ALU.mult, ALU.add)
                ins.then_inc(u_ready, 1)

            def out_stats(b, g, par):
                Gn = GROUPS * b + g
                dve.wait_ge(o_ready, Gn + 1)
                for t in range(GTILES):
                    ins = dve.bn_stats(obn[:, par, t, :], o_ps[par][:, t, :])
                ins.then_inc(obn_ready, 1)
                dve.wait_ge(obn_ready, Gn + 1)
                dve.tensor_tensor(otmp[:, par, 0, :], obn[:, par, :, 1], obn[:, par, :, 4], ALU.subtract)
                dve.tensor_tensor(otmp[:, par, 1, :], obn[:, par, :, 2], obn[:, par, :, 5], ALU.add).then_inc(ovar_step, 1)
                dve.wait_ge(ovar_step, 2 * Gn + 1)
                dve.scalar_tensor_tensor(otmp[:, par, 2, :], otmp[:, par, 0, :], C / 4.0, otmp[:, par, 0, :],
                                         ALU.mult, ALU.mult).then_inc(ovar_step, 1)
                dve.wait_ge(ovar_step, 2 * Gn + 2)
                dve.tensor_tensor(ovar[:, par, :], otmp[:, par, 1, :], otmp[:, par, 2, :], ALU.add).then_inc(ovar_ready, 1)

            def out_rstd(b, g, par):
                Gn = GROUPS * b + g
                dve.wait_ge(ostd_ready, Gn + 1)
                dve.reciprocal(orstd[:, par, :], ostd[:, par, :]).then_inc(orstd_ready, 1)

            def phase2_pair(b, it, more, first=False, last=False):
                for h in range(4):
                    g = 4 * it + h
                    stat = more and not first
                    if not (last and h >= 2):
                        with_positions(b, g + 2, h % 2)
                    out_stats(b, g, h % 2)
                    if stat:
                        unit_stats(b + 1, 2 * it - 2 + h // 2, h // 2, ((h % 2, 0),))
                    out_rstd(b, g, h % 2)
                    if stat:
                        unit_stats(b + 1, 2 * it - 2 + h // 2, h // 2, ((h % 2, 1),))

            def image(b, more):
                group_norm(b)
                normalise(b, 0, 0)
                group_shift(b)
                low_part(b, 0, 0, 0)
                sweep(dve, phase1_group, b)
                inverse_std(b, PAIRS - 2, 2)
                sum_squares(b, PAIRS - 1, 3)
                inverse_std(b, PAIRS - 1, 3)
                for g in range(2):
                    with_positions(b, g, g)
                for g in range(2):
                    low_part(b, 1, g, g)
                mix(b)
                phase2_pair(b, 0, more, first=True)
                with dve.Fori(1, UNITS // 2 - 1) as it:
                    phase2_pair(b, it, more)
                phase2_pair(b, UNITS // 2 - 1, more, last=True)
                if more:
                    unit_stats(b + 1, UNITS - 2, 0)
                    unit_stats(b + 1, UNITS - 1, 1)

            with dve.Fori(0, UNITS // 2) as k:
                unit_stats(0, 2 * k, 0)
                unit_stats(0, 2 * k + 1, 1)
            with dve.Fori(0, B - 1) as b:
                image(b, True)
            image(B - 1, False)

        @block.scalar
        def _(act):
            def high_part(b, phase, g, par):
                H = 2 * GROUPS * b + GROUPS * phase + g
                act.wait_ge(u_ready, H + 1)
                wait_parts_free(act, b, phase, g)
                act.copy(hi[par][:], u[par][:]).then_inc(hi_ready, 1)

            def square(b, p, q):
                Pn = PAIRS * b + p
                act.wait_ge(kv_evac, Pn + 1)
                if not (isinstance(p, int) and p < 2):
                    act.wait_ge(summed, Pn - 1)
                act.activation(sq[q % 2][:].rearrange("p (a c) -> p a c", c=C),
                               kv[q][:].rearrange("p t (a c) -> p (t a) c", a=2)[:, :, 0:C],
                               ACT.Square).then_inc(squared, 1)

            def ones_in_k(b, p, q):
                Pn = PAIRS * b + p
                act.wait_ge(squared, Pn + 1)
                k31 = kv[q][:, :, 0:C].rearrange("p t (h d) -> p t h d", d=DK)[:, :, :, DK - 1]
                act.copy(k31, eps[:, 3:4].unsqueeze(1).broadcast_to([P, 2, HEADS])).then_inc(k_ones, 1)

            def kv_std(b, p, q):
                Pn = PAIRS * b + p
                act.wait_ge(summed, Pn + 1)
                act.activation(std[:, q, :], ssum[:, q, :], ACT.Sqrt, bias=eps[:, 1:2], scale=1.0 / DK).then_inc(std_ready, 1)

            def phase1_group(b, g, par):
                p, q = 2 * g, 2 * par
                first, last = ends(g)
                if not last:
                    high_part(b, 0, g + 1, 1 - par)
                square(b, p, q)
                if not first:
                    kv_std(b, p - 1, (q + 3) % 4)
                ones_in_k(b, p, q)
                square(b, p + 1, q + 1)
                kv_std(b, p, q)
                ones_in_k(b, p + 1, q + 1)

            def normalise_out(b, g, par):
                Gn = GROUPS * b + g
                act.wait_ge(ovar_ready, Gn + 1)
                act.activation(ostd[:, par, :], ovar[:, par, :], ACT.Sqrt, bias=eps[:, 2:3], scale=1.0 / C).then_inc(ostd_ready, 1)
                act.wait_ge(orstd_ready, Gn + 1)
                if not (isinstance(g, int) and g < 2):
                    act.wait_ge(t_ready, Gn - 1)
                for t in range(GTILES):
                    ins = act.activation(z[par][:, t, :], o_ps[par][:, t, :], ACT.Copy, scale=orstd[:, par, t:t + 1])
                ins.then_inc(z_ready, 1)

            def gain_bias(b, g, par):
                Gn = GROUPS * b + g
                act.wait_ge(t_ready, Gn + 1)
                if not (isinstance(g, int) and g < 2):
                    act.wait_ge(y_ready, Gn - 1)
                for c in range(CH):
                    ins = act.activation(wout[par][:, c, :], t_ps[par][:, c, :], ACT.Identity,
                                         bias=cols[:, 4, c:c + 1], scale=cols[:, 3, c:c + 1])
                ins.then_inc(w_ready, 1)

            def phase2_group(b, g, par):
                if not (isinstance(g, int) and g >= GROUPS - 2):
                    high_part(b, 1, g + 2, par)
                if not (isinstance(g, int) and g < 2):
                    gain_bias(b, g - 2, par)
                normalise_out(b, g, par)

            with act.Fori(0, B) as b:
                act.wait_ge(gn_pe, 2 * b + 2)
                act.activation(gstd[:], ps[:, 0, 2:2 + CH], ACT.Sqrt, bias=eps[:, 0:1]).then_inc(gn_act, 1)
                high_part(b, 0, 0, 0)
                sweep(act, phase1_group, b)
                kv_std(b, PAIRS - 1, 3)
                high_part(b, 1, 0, 0)
                high_part(b, 1, 1, 1)
                sweep(act, phase2_group, b, head=4)
                gain_bias(b, GROUPS - 2, 0)
                gain_bias(b, GROUPS - 1, 1)

        @block.gpsimd
        def _(pool):
            pool.wait_ge(max_ready, 1)
            pool.partition_all_reduce(max_all[:], max_in[:], P, bass.bass_isa.ReduceOp.max).then_inc(setup_pool, 1)

            def scale_pair(b, p, q):
                Pn = PAIRS * b + p
                pool.wait_ge(rstd_ready, Pn + 1)
                r = rstd[:, q, :].rearrange("p (t a h) -> p t a h", t=2, a=2)
                k = kv[q][:, :, 0:C].rearrange("p t (h d) -> p t h d", d=DK)[:, :, :, 0:DK - 1]
                pool.tensor_tensor(k, k, r[:, :, 0, :].unsqueeze(3).broadcast_to([P, 2, HEADS, DK - 1]), ALU.mult
                                   ).then_inc(k_scaled, 1)
                v = kv[q][:, :, C + 1:2 * C + 1].rearrange("p t (h d) -> p t h d", d=DK)
                pool.tensor_tensor(v, v, r[:, :, 1, :].unsqueeze(3).broadcast_to([P, 2, HEADS, DK]), ALU.mult
                                   ).then_inc(k_scaled, 1)

            def low_part(b, g, par):
                H = 2 * GROUPS * b + GROUPS + g
                pool.wait_ge(hi_ready, H + 1)
                wait_parts_free(pool, b, 1, g)
                pool.tensor_tensor(lo[par][:], u[par][:], hi[par][:], ALU.subtract).then_inc(lo_ready, 1)

            def residual(b, g, par):
                Gn = GROUPS * b + g
                pool.wait_ge(w_ready, Gn + 1)
                xg = x_group(b, g, par)
                pool.tensor_tensor(xg, xg, wout[par], ALU.add).then_inc(y_ready, 1)

            def phase2_group(b, g, par):
                if not (isinstance(g, int) and g >= GROUPS - 2):
                    low_part(b, g + 2, par)
                if not (isinstance(g, int) and g < 2):
                    residual(b, g - 2, par)

            def ones_beside_v():
                one = eps[:, 3:4].unsqueeze(1).broadcast_to([P, 4, 1])
                for i in range(2):
                    ins = pool.tensor_tensor(kv[i][:].rearrange("p t (a c) -> p (t a) c", a=2)[:, :, C:C + 1],
                                             one, one, ALU.mult)
                ins.then_inc(kv_free, 1)

            with pool.Fori(0, B) as b:
                for q in range(4):
                    scale_pair(b, q, q)
                with pool.Fori(1, PAIRS // 4) as i:
                    for q in range(4):
                        scale_pair(b, 4 * i + q, q)
                sweep(pool, phase2_group, b)
                residual(b, GROUPS - 2, 0)
                residual(b, GROUPS - 1, 1)
                pool.wait_ge(y_ready, GROUPS * b + GROUPS)
                ones_beside_v()

        @block.tensor
        def _(pe):
            pe.wait_ge(params_loaded, 16 * 14)
            for c in range(CH):
                for i, w in enumerate((wk_in, wv_in)):
                    for j in range(CH):
                        mm = pe.transpose(ps[:, c, i * C + j * P:i * C + (j + 1) * P], w[:, j, c * P:(c + 1) * P], ident)
            mm.then_inc(setup_pe, 1)
            pe.wait_ge(wc_ready, 1)
            pe.matmul(ps[:, 2, 0:C], pos[:, 1, :], wc[:, 1, 0:C], start=True, stop=True)
            for h in range(2):
                for d in range(2):
                    mm = pe.matmul(ps[d * HALF:(d + 1) * HALF, 3 + h, 0:C], pos[:, 0, h * HALF:(h + 1) * HALF],
                                   wc[:, 0, 0:C], start=True, stop=True)
            mm.then_inc(setup_pe, 1)
            pe.wait_ge(lmat_ready, 1)
            for j in range(CH):
                pe.matmul(ps[:, 5 + j, 0:C], lmat[:, j, :], wq_in[:, j, :], start=True, stop=True)
                mm = pe.matmul(ps[:, 5 + j, C:C + P], lmat[:, j, :], bq_rep[:, j, :], start=True, stop=True)
            mm.then_inc(setup_pe, 1)

            def project(b, g, t, par, out):
                px = slice(t * W, (t + 1) * W)
                row = g * GTILES + t
                if isinstance(g, int):
                    s = sel[:, row % HALF:row % HALF + 1]
                    r = rowpart[:, row // HALF, :]
                else:
                    s = sel[:, bass.ds(row % HALF, 1)]
                    r = rowpart[:, bass.ds(row // HALF, 1), :].rearrange("p a c -> p (a c)")
                pe.matmul(out, hi[par][:, 0, px], wkv_hi[:, 0, :], start=True, stop=False)
                pe.matmul(out, hi[par][:, 0, px], wkv_lo[:, 0, :], start=False, stop=False)
                pe.matmul(out[:, 0:C], s.broadcast_to([P, P]), r, start=False, stop=False, skip_group_check=True)
                pe.matmul(out, lo[par][:, 0, px], wkv_hi[:, 0, :], start=False, stop=False)
                pe.matmul(out, hi[par][:, 1, px], wkv_hi[:, 1, :], start=False, stop=False)
                pe.matmul(out, hi[par][:, 1, px], wkv_lo[:, 1, :], start=False, stop=False)
                return pe.matmul(out, lo[par][:, 1, px], wkv_hi[:, 1, :], start=False, stop=True)

            def project_pair(b, g, h, par):
                Pn = PAIRS * b + 2 * g + h
                H = 2 * GROUPS * b + g
                if h == 0:
                    pe.wait_ge(lo_ready, H + 1)
                if not (isinstance(g, int) and g == 0):
                    pe.wait_ge(kv_evac, Pn - 1)
                for t in range(2):
                    mm = project(b, g, 2 * h + t, par, kv_ps[h][:, t, :])
                mm.then_inc(kv_proj, 1)

            def scores(b, p, q):
                Pn = PAIRS * b + p
                pe.wait_ge(k_scaled, 2 * Pn + 2)
                pe.wait_ge(k_ones, Pn + 1)
                for t in range(2):
                    for j in range(CH):
                        v0 = C + j * (P + 1)
                        mm = pe.matmul(s_ps[j], kv[q][:, t, j * P:(j + 1) * P], kv[q][:, t, v0:v0 + P + 1],
                                       start=False, stop=False, skip_group_check=True)
                mm.then_inc(scored, 1)

            def phase1_group(b, g, par):
                q = 2 * par
                score = not (isinstance(g, int) and g < 2)
                if score:
                    scores(b, 2 * g - 4, q)
                project_pair(b, g, 0, par)
                if score:
                    scores(b, 2 * g - 3, q + 1)
                project_pair(b, g, 1, par)
                if isinstance(g, int) and g == 1:
                    pe.wait_ge(kv_free, b + 1)
                    for j in range(CH):
                        pe.matmul(s_ps[j], zero16[:, 0:P], zero16[:], start=True, stop=False, skip_group_check=True)

            def project_out(b, g, par):
                H = 2 * GROUPS * b + GROUPS + g
                Gn = GROUPS * b + g
                pe.wait_ge(lo_ready, H + 1)
                if not (isinstance(g, int) and g < 2):
                    pe.wait_ge(z_ready, Gn - 1)
                for t in range(GTILES):
                    px = slice(t * W, (t + 1) * W)
                    out = o_ps[par][:, t, :]
                    first = True
                    for c in range(CH):
                        for st, m in ((hi, m_hi), (hi, m_lo), (lo, m_hi)):
                            pe.matmul(out, st[par][:, c, px], m[:, c, :], start=first, stop=False)
                            first = False
                    mm = pe.matmul(out, ones_hl[:], m_hi[:, 2, :], start=False, stop=True)
                mm.then_inc(o_ready, 1)
                return mm

            def transpose_back(b, g, par):
                Gn = GROUPS * b + g
                pe.wait_ge(z_ready, Gn + 1)
                if not (isinstance(g, int) and g < 2):
                    pe.wait_ge(w_ready, Gn - 1)
                for t in range(GTILES):
                    for c in range(CH):
                        mm = pe.transpose(t_ps[par][:, c, t * W:(t + 1) * W], z[par][:, t, c * P:(c + 1) * P], ident)
                mm.then_inc(t_ready, 1)

            def phase2_group(b, g, par):
                project_out(b, g, par)
                if not (isinstance(g, int) and g < 2):
                    transpose_back(b, g - 2, par)

            with pe.Fori(0, B) as b:
                pe.wait_ge(gn_dve, 8 * b + 1)
                pe.matmul(ps[:, 0, 0:CH], const("blk8"), mv[:, :, 0], start=True, stop=True).then_inc(gn_pe, 1)
                pe.wait_ge(gn_dve, 8 * b + 5)
                pe.matmul(ps[:, 0, 2:2 + CH], const("blk8"), gvar[:], start=True, stop=True).then_inc(gn_pe, 1)
                sweep(pe, phase1_group, b)
                for p in range(PAIRS - 4, PAIRS):
                    scores(b, p, p % 4)
                for j in range(CH):
                    mm = pe.matmul(s_ps[j], zero16[:, 0:P], zero16[:], start=False, stop=True, skip_group_check=True)
                mm.then_inc(sums_done, 1)
                pe.wait_ge(mix_dve, 6 * b + 2)
                for m in range(3):
                    for j in range(CH):
                        st = wql[:, j, m * P:(m + 1) * P] if m < 2 else bql[:, j, :]
                        mm = pe.matmul(ps[:, m, j * P:(j + 1) * P], st, sprime[:, j, :], start=True, stop=True)
                mm.then_inc(mix_pe, 1)
                pe.wait_ge(mix_dve, 6 * b + 6)
                sweep(pe, phase2_group, b, head=4)
                transpose_back(b, GROUPS - 2, 0)
                transpose_back(b, GROUPS - 1, 1)


def _constants():
    import numpy as np
    f = np.float32
    out = np.zeros((P, NCONST), f)

    def put(name, a):
        out[:, CAT[name][0]:CAT[name][1]] = a
    put("ident", np.eye(P, dtype=f))
    same = np.kron(np.eye(P // DK, dtype=f), np.ones((DK, DK), f))
    put("mask", same)
    put("blk8", np.kron(np.eye(P // 8, dtype=f), np.full((8, 8), 0.125, f)))
    rot = np.eye(DK, dtype=f)
    rot[DK - 1, :] = -1
    rot[:, DK - 1] = 0
    one = np.zeros((DK, DK), f)
    one[:, DK - 1] = 1
    put("lrot", np.kron(np.eye(P // DK, dtype=f), rot))
    put("lone", np.kron(np.eye(P // DK, dtype=f), one))
    half = C // 2
    t = (np.arange(1, W + 1, dtype=f) / f(W + 1e-6) * f(2.0 * np.pi)).astype(f)
    dim = np.arange(half, dtype=f)
    dim = (f(10000.0) ** (f(2.0) * np.floor(dim / f(2.0)) / f(half))).astype(f)
    a = (t[None, :] / dim[:, None]).astype(f)
    feat = np.where(np.arange(half)[:, None] % 2 == 0, np.sin(a), np.cos(a)).astype(f)
    put("pos", np.concatenate([feat, feat], axis=1))
    p = np.arange(P)
    put("sel", (p[:, None] % HALF == np.arange(HALF)[None, :]).astype(f))
    put("ones", np.repeat(((p == 0) | (p == 32)).astype(f)[:, None], P, axis=1))
    return out


_INS = ["x", "L0_conv_Wq", "L0_conv_bq", "L0_conv_Wk", "L0_conv_bk", "L0_conv_Wv", "L0_conv_bv", "L0_conv_gK",
        "L0_conv_bK", "L0_conv_gV", "L0_conv_bV", "L0_conv_g_ln", "L0_conv_b_ln"]


def kernel(**inputs):
    import numpy as _np
    import concourse.bacc as _bacc
    from concourse import mybir as _mybir
    from concourse.bass_utils import run_bass_kernel_spmd as _run

    nc = _bacc.Bacc("TRN2", target_bir_lowering=False, num_devices=1)
    arrays, args = {}, []
    for name in _INS:
        a = _np.ascontiguousarray(inputs[name])
        arrays[f"in_{name}_dram"] = a
        args.append(nc.dram_tensor(f"in_{name}_dram", a.shape, _mybir.dt.from_np(a.dtype), kind="ExternalInput").ap())
    arrays["consts_dram"] = _constants()
    args.append(nc.dram_tensor("consts_dram", (P, NCONST), _mybir.dt.float32, kind="ExternalInput").ap())
    args.append(nc.dram_tensor("out_0_dram", (B, C, ROWS, W), _mybir.dt.float32, kind="ExternalOutput").ap())
    build(nc, *args)
    r = _run(nc, [arrays], core_ids=[0])
    return r.results[0]["out_0_dram"]
```

```python
from contextlib import ExitStack

import concourse.bass as bass
from concourse import mybir

ALU = mybir.AluOpType
ACT = mybir.ActivationFunctionType
F32 = mybir.dt.float32
F16 = mybir.dt.float16
AX = mybir.AxisListType

P = 128
B = 8
C = 256
CH = C // P
W = 128
ROWS = 128
NPIX = ROWS * W
HEADS = 8
DK = C // HEADS
HPC = HEADS // CH
GTILES = 4
GPIX = GTILES * W
GROUPS = ROWS // GTILES
PAIRS = 2 * GROUPS
SPARE = 4
SLOTS = GROUPS + SPARE
NGROUPS = B * GROUPS
HALF = ROWS // 2
EPS = 1e-5
KVR = 4
VROW = C + 1 + C + 1
WBOUND = 64.0
MBOUND = 32768.0

CONSTS = [("ident", P), ("blk8", P), ("pos", 2 * P), ("lrot", P), ("lone", P), ("mask", P), ("sel", HALF), ("ones", P)]
CAT = {}
_at = 0
for _name, _n in CONSTS:
    CAT[_name] = (_at, _at + _n)
    _at += _n
NCONST = _at
NKEPT = CAT["pos"][1]


def slots_from(eng, n0, step):
    found = {}

    def slot(j):
        a = j - j % step
        if a not in found:
            found[a] = eng.snap((n0 + a) % SLOTS)
        return found[a] + j % step
    return slot


def sweep(eng, body, b, head=2, tail=2):
    def run(g0, groups):
        slot = slots_from(eng, GROUPS * b + g0, 2)
        for h in groups:
            body(b, g0 + h, h % 2, lambda d, h=h: slot(h + d))
    run(0, range(head))
    with eng.Fori(head // 2, (GROUPS - tail) // 2) as i:
        run(2 * i, range(2))
    run(GROUPS - tail, range(tail))


def ends(g):
    return (isinstance(g, int) and g == 0, isinstance(g, int) and g == GROUPS - 1)


def build(nc, x, Wq, bq, Wk, bk, Wv, bv, gK, bK, gV, bV, g_ln, b_ln, consts, y):
    with ExitStack() as ctx:
        def sb(name, shape, dt=F32):
            return ctx.enter_context(nc.sbuf_tensor(name, shape, dt))

        def sem(name):
            return ctx.enter_context(nc.semaphore(name))

        xr = sb("x_ring", [P, SLOTS, CH, GPIX])
        wkv_hi = sb("wkv_hi", [P, CH, 2 * C], F16)
        wkv_lo = sb("wkv_lo", [P, CH, 2 * C], F16)
        rowpart = sb("rowpart", [P, 2, C], F16)
        sel = sb("sel", [P, HALF], F16)
        ones_hl = sb("ones_hl", [P, P], F16)
        kv_add = sb("kv_add", [P, 2 * C])
        cst = sb("cst", [P, NKEPT])
        posb = sb("posb", [P, CH, P])
        wql = sb("wql", [P, CH, C])
        bql = sb("bql", [P, CH, P])
        gvm = sb("gvm", [P, CH, P])
        bvm = sb("bvm", [P, CH, P])
        cols = sb("cols", [P, 5, CH])
        sprime = sb("sprime", [P, CH, P + 1])
        m_hi = sb("m_hi", [P, 3, C], F16)
        m_lo = sb("m_lo", [P, 2, C], F16)
        u = [sb(f"u{i}", [P, CH, GPIX]) for i in range(2)]
        hi = [sb(f"hi{i}", [P, CH, GPIX], F16) for i in range(2)]
        lo = [sb(f"lo{i}", [P, CH, GPIX], F16) for i in range(2)]
        kv = [sb(f"kv{i}", [P, 2, VROW]) for i in range(KVR)]
        sq = [sb(f"sq{i}", [P, 2 * 2 * C]) for i in range(2)]
        ssum = sb("ssum", [P, 4, 2 * 2 * HEADS])
        std = sb("std", [P, 4, 2 * 2 * HEADS])
        rstd = sb("rstd", [P, 4, 2 * 2 * HEADS])
        stats = sb("stats", [P, CH, GROUPS, 6])
        obn = sb("obn", [P, 2, GTILES, 6])
        omv = sb("omv", [P, 2, GTILES, 2])
        ostd = sb("ostd", [P, 2, GTILES])
        orstd = sb("orstd", [P, 2, GTILES])
        mv = sb("mv", [P, CH, 2])
        gmean = sb("gmean", [P, CH])
        gdev = sb("gdev", [P, CH])
        gsq = sb("gsq", [P, CH])
        gvar = sb("gvar", [P, CH])
        gstd = sb("gstd", [P, CH])
        grstd = sb("grstd", [P, CH])
        gshift = sb("gshift", [P, CH])
        eps = sb("eps", [P, 4])
        small = sb("small", [P, 32])
        max_in = sb("max_in", [P, 8])
        max_all = sb("max_all", [P, 8])
        zero16 = sb("zero16", [P, P + 1], F16)
        mmean = sb("mmean", [P, 4])
        z = [s[:].rearrange("p (t c) -> p t c", t=GTILES) for s in sq]
        wout = [t[:].rearrange("p a b -> p (a b)")[:, 0:CH * GPIX].rearrange("p (c t) -> p c t", c=CH) for t in kv[0:2]]
        TEMP_SLOT = SLOTS - 12
        flat = xr[:].rearrange("p s c t -> p (s c t)")[:, TEMP_SLOT * CH * GPIX:]

        def temp(i, n):
            return flat[:, i * 1024:i * 1024 + n]
        wk_in = temp(0, 2 * C).rearrange("p (j c) -> p j c", j=CH)
        wv_in = temp(1, 2 * C).rearrange("p (j c) -> p j c", j=CH)
        wq_in = temp(2, 2 * C).rearrange("p (j c) -> p j c", j=CH)
        bias_in = temp(3, 2 * C)
        gv_in = temp(4, 2 * C)
        wt = temp(5, 1024).rearrange("p (c d) -> p c d", c=CH)
        wc = temp(6, 1024).rearrange("p (c d) -> p c d", c=CH)
        lmat = temp(7, CH * P).rearrange("p (j d) -> p j d", j=CH)
        lone_g = temp(8, CH * P).rearrange("p (j d) -> p j d", j=CH)
        bias_c = temp(9, 2 * C)
        bq_rep = temp(10, CH * P).rearrange("p (j d) -> p j d", j=CH)
        cst_setup = temp(11, NCONST - NKEPT)
        s_gain = sq[1][:, 0:CH * P].rearrange("p (j d) -> p j d", j=CH)

        ps = ctx.enter_context(nc.psum_tensor("ps", [P, 8, 512], F32))
        kv_ps = [ps[:, 2 * i:2 * i + 2, :] for i in range(2)]
        o_ps = [ps[:, 2 * i:2 * i + 2, :].rearrange("p a (t c) -> p (a t) c", t=2) for i in range(2)]
        m_ps = ps[:, 0:3, :].rearrange("p m (j d) -> p m j d", j=CH)
        s_ps = [ps[:, 4 + j, 0:P + 1] for j in range(CH)]
        t_ps = [ps[:, 4 + 2 * i:6 + 2 * i, :] for i in range(2)]

        def const(name):
            a, b_ = CAT[name]
            return cst[:, a:b_] if b_ <= NKEPT else cst_setup[:, a - NKEPT:b_ - NKEPT]
        ident = const("ident")
        pos = const("pos").rearrange("p (c t) -> p c t", c=CH)

        params_loaded = sem("params_loaded")
        loaded = [sem(f"loaded{i}") for i in range(4)]
        stored = [sem(f"stored{i}") for i in range(2)]
        setup_dve = sem("setup_dve")
        setup_pe = sem("setup_pe")
        setup_pool = sem("setup_pool")
        max_ready = sem("max_ready")
        wc_ready = sem("wc_ready")
        lmat_ready = sem("lmat_ready")
        ring_free = sem("ring_free")
        stats_done = sem("stats_done")
        gn_dve = sem("gn_dve")
        gn_pe = sem("gn_pe")
        gn_act = sem("gn_act")
        u_ready = sem("u_ready")
        hi_ready = sem("hi_ready")
        lo_ready = sem("lo_ready")
        kv_proj = sem("kv_proj")
        kv_evac = sem("kv_evac")
        tile_evac = sem("tile_evac")
        tile_squared = sem("tile_squared")
        squared = sem("squared")
        k_ones = sem("k_ones")
        summed = sem("summed")
        std_ready = sem("std_ready")
        rstd_ready = sem("rstd_ready")
        scaled = sem("scaled")
        last_v_scaled = sem("last_v_scaled")
        scored = sem("scored")
        sums_done = sem("sums_done")
        kv_free = sem("kv_free")
        mix_dve = sem("mix_dve")
        mix_pe = sem("mix_pe")
        mix_act = sem("mix_act")
        o_ready = sem("o_ready")
        obn_ready = sem("obn_ready")
        ovar_ready = sem("ovar_ready")
        ostd_ready = sem("ostd_ready")
        orstd_ready = sem("orstd_ready")
        z_ready = sem("z_ready")
        t_ready = sem("t_ready")
        w_ready = sem("w_ready")
        y_ready = sem("y_ready")
        late_added = sem("late_added")

        x_dram = x.rearrange("b (c p) (k r) w -> b k p c (r w)", p=P, k=GROUPS)
        y_dram = y.rearrange("b (c p) (k r) w -> b k p c (r w)", p=P, k=GROUPS)

        def dram_group(t, n):
            if isinstance(n, int):
                return t[n // GROUPS, n % GROUPS]
            return t[bass.ds(n // GROUPS, 1), bass.ds(n % GROUPS, 1)].rearrange("a k p c t -> p (a k c) t")

        def in_ring(s):
            if isinstance(s, int):
                return xr[:, s]
            return xr[:, bass.ds(s, 1)].rearrange("p a c t -> p (a c) t")

        def wait_parts_free(eng, b, phase, g):
            if phase == 0:
                if not (isinstance(g, int) and g < 2):
                    eng.wait_ge(kv_proj, PAIRS * b + 2 * g - 2)
            elif isinstance(g, int) and g < 2:
                eng.wait_ge(kv_proj, PAIRS * b + PAIRS)
            else:
                eng.wait_ge(o_ready, GROUPS * b + g - 1)

        block = ctx.enter_context(nc.Block())

        @block.sync
        def _(sp):
            def load(n, q):
                if not isinstance(n, int) or n >= 4:
                    sp.wait_ge(loaded[q], (n - q) // 4 * 16)
                sp.dma_start(in_ring(n % SLOTS), dram_group(x_dram, n)).then_inc(loaded[q], 16)

            def store(m, q):
                sp.wait_ge(y_ready, m + 1)
                sp.dma_start(dram_group(y_dram, m), in_ring(m % SLOTS)).then_inc(stored[q % 2], 16)

            def refill(m, q):
                sp.wait_ge(stored[q % 2], (m - q % 2) // 2 * 16 + 16)
                load(m + SLOTS, q)

            def store_and_refill(m, q):
                store(m, q)
                refill(m - 1, (q - 1) % 4)

            def run(m0, steps):
                store(m0, 0)
                for h in range(1, 4):
                    store_and_refill(m0 + h, h)
                with sp.Fori(1, steps // 4) as i:
                    for h in range(4):
                        store_and_refill(m0 + 4 * i + h, h)
                refill(m0 + steps - 1, 3)

            sp.dma_start(cst[:], consts[:, 0:NKEPT]).then_inc(params_loaded, 16)
            sp.dma_start(cst_setup, consts[:, NKEPT:NCONST]).then_inc(params_loaded, 16)
            for dst, src in ((wk_in, Wk), (wv_in, Wv), (wq_in, Wq)):
                sp.dma_start(dst, src.rearrange("(j p) c -> p j c", p=P)).then_inc(params_loaded, 16)
            for i, src in enumerate((bk, bv)):
                sp.dma_start(bias_in[:, i * C:(i + 1) * C], src.rearrange("(a c) -> a c", a=1).partition_broadcast(P)
                             ).then_inc(params_loaded, 16)
            for i, src in enumerate((gV, bV)):
                sp.dma_start(gv_in[:, i * C:(i + 1) * C],
                             src.rearrange("h d -> (h d)").rearrange("(a c) -> a c", a=1).partition_broadcast(P)
                             ).then_inc(params_loaded, 16)
            for i, src in enumerate((gK.rearrange("h d -> (h d)"), bK.rearrange("h d -> (h d)"), bq, g_ln, b_ln)):
                sp.dma_start(cols[:, i, :], src.rearrange("(j p) -> p j", p=P), allow_slow_non_contiguous=True
                             ).then_inc(params_loaded, 16)
            for n in range(SLOTS):
                if n == TEMP_SLOT:
                    sp.wait_ge(ring_free, 1)
                load(n, n % 4)
            run(0, GROUPS - SPARE)
            with sp.Fori(1, B - 1) as b:
                run(GROUPS * b - SPARE, GROUPS)
            for m in range(NGROUPS - SLOTS, NGROUPS):
                store(m, m % 4)
            sp.wait_ge(stored[0], NGROUPS // 2 * 16)
            sp.wait_ge(stored[1], NGROUPS // 2 * 16)

        @block.vector
        def _(dve):
            step = [0]

            def link(ins):
                step[0] += 1
                ins.then_inc(setup_dve, 1)
                dve.wait_ge(setup_dve, step[0])
            dve.wait_ge(params_loaded, 16 * 14)
            dve.tensor_copy(sel[:], const("sel"))
            dve.tensor_copy(ones_hl[:], const("ones"))
            dve.memset(m_hi[:], 0.0)
            dve.memset(zero16[:], 0.0)
            for t in kv:
                ins = dve.memset(t[:], 1.0)
            ins.then_inc(kv_free, 1)
            dve.memset(eps[:, 0:3], EPS)
            dve.memset(eps[:, 3:4], 1.0)
            dve.wait_ge(setup_pe, 1)
            link(dve.tensor_copy(wt, ps[:, 0:CH, :]))
            wt_h = wt.rearrange("p c (h d) -> p c h d", d=DK)
            hm = small[:, 0:32].rearrange("p (c h) -> p c h", c=CH)
            link(dve.tensor_reduce(hm, wt_h, AX.X, ALU.add))
            link(dve.tensor_scalar(small[:, 0:32], small[:, 0:32], -1.0 / DK, None, ALU.mult))
            for c in range(CH):
                ins = dve.tensor_tensor(wc[:, c, :].rearrange("p (h d) -> p h d", d=DK), wt_h[:, c],
                                        hm[:, c, :].unsqueeze(2).broadcast_to([P, 16, DK]), ALU.add)
            link(ins)
            bias_h = bias_in.rearrange("p (h d) -> p h d", d=DK)
            link(dve.tensor_reduce(small[:, 0:16], bias_h, AX.X, ALU.add))
            link(dve.tensor_scalar(small[:, 0:16], small[:, 0:16], -1.0 / DK, None, ALU.mult))
            link(dve.tensor_tensor(bias_c.rearrange("p (h d) -> p h d", d=DK), bias_h,
                                   small[:, 0:16].unsqueeze(2).broadcast_to([P, 16, DK]), ALU.add))
            link(dve.memset(small[:], 0.0))

            def absmax(col, src):
                return dve.tensor_reduce(small[:, col:col + 1], src, AX.XY, ALU.max, apply_absolute_value=True)
            absmax(0, wc)
            absmax(1, wq_in)
            for col, src in ((2, cols[:, 0:1, :]), (3, cols[:, 1:2, :]), (6, cols[:, 2:3, :])):
                absmax(col, src)
            absmax(4, gv_in[:, 0:C].rearrange("p (a c) -> p a c", a=1))
            link(absmax(5, gv_in[:, C:2 * C].rearrange("p (a c) -> p a c", a=1)))
            link(dve.tensor_tensor(small[:, 1:2], small[:, 1:2], small[:, 6:7], ALU.max))
            dve.tensor_copy(max_in[:], small[:, 0:8]).then_inc(max_ready, 1)
            dve.wait_ge(setup_pool, 1)
            link(dve.tensor_scalar(small[:, 8:16], max_all[:], 1e-12, None, ALU.max))
            link(dve.scalar_tensor_tensor(small[:, 16:17], small[:, 10:11], float(DK) ** 0.5, small[:, 11:12], ALU.mult, ALU.add))
            link(dve.scalar_tensor_tensor(small[:, 17:18], small[:, 12:13], float(DK) ** 0.5, small[:, 13:14], ALU.mult, ALU.add))
            link(dve.tensor_scalar(small[:, 16:18], small[:, 16:18], 1e-3, None, ALU.max))
            link(dve.tensor_tensor(small[:, 18:19], small[:, 16:17], small[:, 17:18], ALU.mult))
            link(dve.tensor_tensor(small[:, 19:20], small[:, 18:19], small[:, 9:10], ALU.mult))
            link(dve.reciprocal(small[:, 20:21], small[:, 8:9]))
            link(dve.reciprocal(small[:, 21:22], small[:, 19:20]))
            link(dve.tensor_scalar(small[:, 22:23], small[:, 20:21], WBOUND, None, ALU.mult))
            link(dve.tensor_scalar(small[:, 23:24], small[:, 21:22], MBOUND / (2 * DK), None, ALU.mult))
            link(dve.tensor_scalar(small[:, 24:25], small[:, 23:24], 1.0 / NPIX, None, ALU.mult))
            link(dve.tensor_scalar(eps[:, 1:2], small[:, 22:23], small[:, 22:23], EPS, ALU.mult, ALU.mult))
            link(dve.tensor_scalar(eps[:, 2:3], small[:, 23:24], small[:, 23:24], EPS / 4, ALU.mult, ALU.mult))
            link(dve.tensor_scalar(wc, wc, small[:, 22:23], None, ALU.mult))
            link(dve.tensor_scalar(bias_c, bias_c, small[:, 22:23], None, ALU.mult))
            dve.tensor_copy(wkv_hi[:], wc).then_inc(wc_ready, 1)
            dve.wait_ge(wc_ready, 1)
            link(dve.tensor_tensor(wkv_lo[:], wc, wkv_hi[:], ALU.subtract))
            for j in range(CH):
                ins = dve.tensor_scalar(lone_g[:, j, :], const("lone"), cols[:, 1, j:j + 1], None, ALU.mult)
            link(ins)
            for j in range(CH):
                dve.scalar_tensor_tensor(lmat[:, j, :], const("lrot"), cols[:, 0, j:j + 1], lone_g[:, j, :], ALU.mult, ALU.add)
            for j in range(CH):
                dve.tensor_copy(bq_rep[:, j, :], cols[:, 2, j:j + 1].broadcast_to([P, P]))
                for t, o in ((gvm, 0), (bvm, C)):
                    ins = dve.tensor_tensor(t[:, j, :], gv_in[:, o + j * P:o + (j + 1) * P], const("mask"), ALU.mult)
            ins.then_inc(lmat_ready, 1)
            dve.wait_ge(setup_pe, 2)
            dve.tensor_tensor(kv_add[:, 0:C], ps[:, 2, 0:C], bias_c[:, 0:C], ALU.add)
            dve.tensor_copy(kv_add[:, C:2 * C], bias_c[:, C:2 * C])
            for h in range(2):
                dve.tensor_copy(rowpart[0:HALF, h, :], ps[0:HALF, 3 + h, 0:C])
                link(dve.tensor_copy(sq[0][HALF:P, h * C:h * C + C // 2].bitcast(F16), ps[HALF:P, 3 + h, 0:C]))
                link(dve.tensor_tensor(rowpart[HALF:P, h, :], ps[HALF:P, 3 + h, 0:C],
                                       sq[0][HALF:P, h * C:h * C + C // 2].bitcast(F16), ALU.subtract))
            dve.wait_ge(setup_pe, 3)
            for j in range(CH):
                dve.tensor_scalar(wql[:, j, :], ps[:, 5 + j, 0:C], small[:, 24:25], None, ALU.mult)
                ins = dve.tensor_scalar(bql[:, j, :], ps[:, 5 + j, C:C + P], small[:, 24:25], None, ALU.mult)
            link(ins)
            dve.drain().then_inc(ring_free, 1)

            def group_stats(b, k, h, s):
                g = 4 * k + h
                xg = in_ring(s)
                if isinstance(g, int):
                    dst = [stats[:, c, g, :] for c in range(CH)]
                else:
                    dst = [stats[:, c, bass.ds(g, 1), :].rearrange("p a s -> p (a s)") for c in range(CH)]
                dve.wait_ge(loaded[h], 16 * (GROUPS // 4 * b + k) + 16)
                return lambda c: dve.bn_stats(dst[c], xg[:, c, :]).then_inc(stats_done, 1)

            def all_stats(b, k, h, s):
                chunk_stats = group_stats(b, k, h, s)
                for c in range(CH):
                    chunk_stats(c)

            def group_norm(b):
                G = 8
                dve.wait_ge(stats_done, CH * GROUPS * b + CH * GROUPS)
                dve.memset(mmean[:, 3:4], 0.0)
                for c in range(CH):
                    ins = dve.bn_aggr(mv[:, c, :], stats[:, c].rearrange("p g s -> p (g s)"))
                ins.then_inc(gn_dve, 1)
                dve.wait_ge(gn_pe, 2 * b + 1)
                dve.tensor_tensor(gdev[:], mv[:, :, 0], ps[:, 0, 0:CH], ALU.subtract).then_inc(gn_dve, 1)
                dve.tensor_copy(gmean[:], ps[:, 0, 0:CH]).then_inc(gn_dve, 1)
                dve.wait_ge(gn_dve, G * b + 2)
                dve.tensor_tensor(gsq[:], gdev[:], gdev[:], ALU.mult).then_inc(gn_dve, 1)
                dve.wait_ge(gn_dve, G * b + 4)
                dve.tensor_tensor(gvar[:], gsq[:], mv[:, :, 1], ALU.add).then_inc(gn_dve, 1)
                dve.wait_ge(gn_act, b + 1)
                dve.reciprocal(grstd[:], gstd[:]).then_inc(gn_dve, 1)
                dve.wait_ge(gn_dve, G * b + 6)

            def group_shift(b):
                G = 8
                dve.scalar_tensor_tensor(gshift[:], gmean[:], -1.0, grstd[:], ALU.mult, ALU.mult).then_inc(gn_dve, 1)
                dve.wait_ge(kv_free, b + 1)
                dve.wait_ge(gn_dve, G * b + 7)
                for c in range(CH):
                    ins = dve.tensor_scalar(posb[:, c, :], pos[:, c, :], gshift[:, c:c + 1], None, ALU.add)
                ins.then_inc(gn_dve, 1)
                dve.wait_ge(gn_dve, G * b + 8)

            def normalise(b, g, par, s):
                H = 2 * GROUPS * b + g
                if not (isinstance(g, int) and g < 2):
                    dve.wait_ge(hi_ready, H - 1)
                xg = in_ring(s)
                for c in range(CH):
                    ins = dve.tensor_scalar(u[par][:, c, :], xg[:, c, :], gmean[:, c:c + 1], grstd[:, c:c + 1],
                                            ALU.subtract, ALU.mult)
                ins.then_inc(u_ready, 1)

            def low_part(b, g, par):
                H = 2 * GROUPS * b + g
                dve.wait_ge(hi_ready, H + 1)
                wait_parts_free(dve, b, 0, g)
                dve.tensor_tensor(lo[par][:], u[par][:], hi[par][:], ALU.subtract).then_inc(lo_ready, 1)

            def evacuate(b, p, q):
                Pn = PAIRS * b + p
                dve.wait_ge(kv_proj, Pn + 1)
                if not (isinstance(p, int) and p < KVR):
                    dve.wait_ge(scored, Pn - KVR + 1)
                dst = kv[q][:].rearrange("p t (a c) -> p t a c", a=2)[:, :, :, 0:C]
                src = kv_ps[q % 2].rearrange("p t (a c) -> p t a c", a=2)
                add = kv_add[:].rearrange("p (a c) -> p a c", a=2).unsqueeze(1).broadcast_to([P, 2, 2, C])
                dve.tensor_tensor(dst, src, add, ALU.add).then_inc(kv_evac, 1)

            def evacuate_tiles(b, p, q):
                Pn = PAIRS * b + p
                dve.wait_ge(kv_proj, Pn + 1)
                dve.wait_ge(scored, Pn - KVR + 1)
                add = kv_add[:].rearrange("p (a c) -> p a c", a=2)
                for t, done in ((0, tile_evac), (1, kv_evac)):
                    dve.tensor_tensor(kv[q][:, t, :].rearrange("p (a c) -> p a c", a=2)[:, :, 0:C],
                                      kv_ps[q % 2][:, t, :].rearrange("p (a c) -> p a c", a=2), add, ALU.add
                                      ).then_inc(done, 1)

            def sum_tiles(b, p, q):
                S = 2 * HEADS
                for t, ready, n in ((0, tile_squared, b + 1), (1, squared, PAIRS * b + p + 1)):
                    dve.wait_ge(ready, n)
                    ins = dve.tensor_reduce(ssum[:, q, t * S:(t + 1) * S],
                                            sq[q % 2][:, 2 * C * t:2 * C * (t + 1)].rearrange("p (h d) -> p h d", d=DK),
                                            AX.X, ALU.add)
                ins.then_inc(summed, 1)

            def sum_squares(b, p, q):
                Pn = PAIRS * b + p
                dve.wait_ge(squared, Pn + 1)
                dve.tensor_reduce(ssum[:, q, :], sq[q % 2][:].rearrange("p (h d) -> p h d", d=DK),
                                  AX.X, ALU.add).then_inc(summed, 1)

            def inverse_std(b, p, q):
                Pn = PAIRS * b + p
                dve.wait_ge(std_ready, Pn + 1)
                dve.reciprocal(rstd[:, q, :], std[:, q, :]).then_inc(rstd_ready, 1)

            def phase1_group(b, g, par, slot):
                p, q = 2 * g, 2 * par
                first, last = ends(g)
                if last:
                    sum_squares(b, p - 1, (q + 3) % 4)
                    inverse_std(b, p - 2, (q + 2) % 4)
                    evacuate(b, p, q)
                    inverse_std(b, p - 1, (q + 3) % 4)
                    scale_v(b, p - 1, (q + 3) % 4)
                    sum_squares(b, p, q)
                    evacuate_tiles(b, p + 1, q + 1)
                    inverse_std(b, p, q)
                    sum_tiles(b, p + 1, q + 1)
                    scale_v(b, p, q)
                    inverse_std(b, p + 1, q + 1)
                    scale_v(b, p + 1, q + 1)
                    return
                normalise(b, g + 1, 1 - par, slot(1))
                if not first:
                    inverse_std(b, p - 2, (q + 2) % 4)
                evacuate(b, p, q)
                if not first:
                    sum_squares(b, p - 1, (q + 3) % 4)
                low_part(b, g + 1, 1 - par)
                if not first:
                    inverse_std(b, p - 1, (q + 3) % 4)
                evacuate(b, p + 1, q + 1)
                sum_squares(b, p, q)

            def scale_v(b, p, q):
                dve.wait_ge(rstd_ready, PAIRS * b + p + 1)
                v = kv[q][:, :, C + 1:2 * C + 1].rearrange("p t (h d) -> p t h d", d=DK)
                r = rstd[:, q, :].rearrange("p (t a h) -> p t a h", t=2, a=2)
                dve.tensor_tensor(v, v, r[:, :, 1, :].unsqueeze(3).broadcast_to([P, 2, HEADS, DK]), ALU.mult
                                  ).then_inc(last_v_scaled, 1)

            def mix(b, meanwhile):
                N = 6
                dve.wait_ge(sums_done, b + 1)
                for j in range(CH):
                    v0, one = (1, 0) if j == 0 else (0, P)
                    dve.tensor_tensor(s_gain[:, j, :], s_ps[j][:, v0:v0 + P], gvm[:, j, :], ALU.mult)
                    ins = dve.tensor_copy(mmean[:, j:j + 1], s_ps[j][:, one:one + 1])
                ins.then_inc(mix_dve, 1)
                dve.wait_ge(mix_dve, N * b + 1)
                for j in range(CH):
                    ins = dve.scalar_tensor_tensor(sprime[:, j, 0:P], bvm[:, j, :], mmean[:, j:j + 1], s_gain[:, j, :],
                                                   ALU.mult, ALU.add)
                ins.then_inc(mix_dve, 1)
                dve.wait_ge(mix_dve, N * b + 2)
                dve.tensor_reduce(mmean[:, 0:CH], sprime[:, :, 0:P], AX.X, ALU.add).then_inc(mix_dve, 1)
                dve.wait_ge(mix_dve, N * b + 3)
                dve.tensor_scalar(sprime[:, :, P], mmean[:, 0:CH], -1.0 / C, None, ALU.mult).then_inc(mix_dve, 1)
                meanwhile()
                dve.wait_ge(mix_pe, b + 1)
                dve.tensor_reduce(mmean[:, 0:3], m_ps[:, :, :, P], AX.X, ALU.add).then_inc(mix_dve, 1)
                for i, m in enumerate((2, 0, 1)):
                    dve.wait_ge(mix_act, 3 * b + i + 1)
                    rows = slice(0, P) if m < 2 else slice(32, 64)
                    high = m_hi[rows, m, :].rearrange("p (j d) -> p j d", j=CH)
                    low = m_lo[:, m, :].rearrange("p (j d) -> p j d", j=CH) if m < 2 else high
                    ins = dve.scalar_tensor_tensor(low, m_ps[rows, m, :, 0:P], mmean[rows, m:m + 1], high,
                                                   ALU.add, ALU.subtract)
                ins.then_inc(mix_dve, 1)

            def with_positions(b, g, par, s, between=lambda: None):
                H = 2 * GROUPS * b + GROUPS + g
                xg = in_ring(s)
                row = bass.ds(g * GTILES, GTILES)
                add0 = posb[:, 0, row].unsqueeze(2).broadcast_to([P, GTILES, W])
                add1 = posb[:, 1, :].unsqueeze(1).broadcast_to([P, GTILES, W])
                dve.wait_ge(lo_ready, H - 1)
                for c, add in ((0, add0), (1, add1)):
                    if c == 1:
                        between()
                    ins = dve.scalar_tensor_tensor(u[par][:, c, :].rearrange("p (r w) -> p r w", w=W),
                                                   xg[:, c, :].rearrange("p (r w) -> p r w", w=W),
                                                   grstd[:, c:c + 1], add, ALU.mult, ALU.add)
                ins.then_inc(u_ready, 1)

            def out_stats(b, g, par, between):
                Gn = GROUPS * b + g
                dve.wait_ge(o_ready, Gn + 1)
                for t in range(GTILES):
                    ins = dve.bn_stats(obn[:, par, t, :], o_ps[par][:, t, :])
                ins.then_inc(obn_ready, 1)
                between()
                dve.wait_ge(obn_ready, Gn + 1)
                dve.memset(mmean[:, 3:4], 0.0)
                for t in range(GTILES):
                    ins = dve.bn_aggr(omv[:, par, t, :], obn[:, par, t, :])
                ins.then_inc(ovar_ready, 1)

            def out_rstd(b, g, par):
                Gn = GROUPS * b + g
                dve.wait_ge(ostd_ready, Gn + 1)
                dve.reciprocal(orstd[:, par, :], ostd[:, par, :]).then_inc(orstd_ready, 1)

            def late_residual(b, g, par, s):
                dve.wait_ge(w_ready, GROUPS * b + g + 1)
                xg = in_ring(s)[:, 1, :]
                dve.tensor_tensor(xg, xg, wout[par][:, 1, :], ALU.add).then_inc(late_added, 1)

            def phase2_four(b, it, more, first=False, last=False):
                slot = slots_from(dve, GROUPS * b + 4 * it, 4)
                for h in range(4):
                    g = 4 * it + h
                    stat = more and not (first and h < 2)
                    if stat:
                        k, r = (it - 1, h + 2) if h < 2 else (it, h - 2)
                        s = slot(GROUPS + h - 2)
                        chunk_stats = group_stats(b + 1, k, r, s)
                        out_stats(b, g, h % 2, lambda: chunk_stats(0))
                        chunk_stats(1)
                    else:
                        out_stats(b, g, h % 2, lambda: None)
                    if last and h >= 1:
                        out_rstd(b, g, h % 2)
                        late_residual(b, g - 2, h % 2, slot(h - 2))
                    else:
                        with_positions(b, g + 3, (h + 1) % 2, slot(h + 3), lambda: out_rstd(b, g, h % 2))

            def image(b, more):
                slot = slots_from(dve, GROUPS * b, 4)
                first_three = (slot(0), slot(1), slot(2))
                group_norm(b)
                normalise(b, 0, 0, first_three[0])
                group_shift(b)
                low_part(b, 0, 0)
                sweep(dve, phase1_group, b)
                with_positions(b, 0, 0, first_three[0])
                mix(b, lambda: with_positions(b, 1, 1, first_three[1]))
                with_positions(b, 2, 0, first_three[2])
                phase2_four(b, 0, more, first=True)
                with dve.Fori(1, GROUPS // 4 - 1) as it:
                    phase2_four(b, it, more)
                phase2_four(b, GROUPS // 4 - 1, more, last=True)
                if more:
                    slot = slots_from(dve, GROUPS * b, 4)
                    for h in (2, 3):
                        all_stats(b + 1, GROUPS // 4 - 1, h, slot(2 * GROUPS - 4 + h))

            with dve.Fori(0, GROUPS // 4) as k:
                for h in range(4):
                    all_stats(0, k, h, 4 * k + h)
            with dve.Fori(0, B - 1) as b:
                image(b, True)
            image(B - 1, False)

        @block.scalar
        def _(act):
            def high_part(b, phase, g, par):
                H = 2 * GROUPS * b + GROUPS * phase + g
                act.wait_ge(u_ready, H + 1)
                wait_parts_free(act, b, phase, g)
                act.copy(hi[par][:], u[par][:]).then_inc(hi_ready, 1)

            def square(b, p, q):
                Pn = PAIRS * b + p
                act.wait_ge(kv_evac, Pn + 1)
                if not (isinstance(p, int) and p < 2):
                    act.wait_ge(summed, Pn - 1)
                act.activation(sq[q % 2][:].rearrange("p (a c) -> p a c", c=C),
                               kv[q][:].rearrange("p t (a c) -> p (t a) c", a=2)[:, :, 0:C],
                               ACT.Square).then_inc(squared, 1)

            def square_tiles(b, p, q):
                Pn = PAIRS * b + p
                for t, ready, n, done in ((0, tile_evac, b + 1, tile_squared), (1, kv_evac, Pn + 1, squared)):
                    act.wait_ge(ready, n)
                    if t == 0:
                        act.wait_ge(summed, Pn - 1)
                    act.activation(sq[q % 2][:, 2 * C * t:2 * C * (t + 1)].rearrange("p (a c) -> p a c", c=C),
                                   kv[q][:, t, :].rearrange("p (a c) -> p a c", a=2)[:, :, 0:C],
                                   ACT.Square).then_inc(done, 1)

            def ones_in_k(b, p, q):
                Pn = PAIRS * b + p
                act.wait_ge(squared, Pn + 1)
                k31 = kv[q][:, :, 0:C].rearrange("p t (h d) -> p t h d", d=DK)[:, :, :, DK - 1]
                act.copy(k31, eps[:, 3:4].unsqueeze(1).broadcast_to([P, 2, HEADS])).then_inc(k_ones, 1)

            def kv_std(b, p, q):
                Pn = PAIRS * b + p
                act.wait_ge(summed, Pn + 1)
                act.activation(std[:, q, :], ssum[:, q, :], ACT.Sqrt, bias=eps[:, 1:2], scale=1.0 / DK).then_inc(std_ready, 1)

            def phase1_group(b, g, par, slot):
                p, q = 2 * g, 2 * par
                first, last = ends(g)
                if last:
                    kv_std(b, p - 1, (q + 3) % 4)
                    square(b, p, q)
                    ones_in_k(b, p, q)
                    kv_std(b, p, q)
                    square_tiles(b, p + 1, q + 1)
                    kv_std(b, p + 1, q + 1)
                    ones_in_k(b, p + 1, q + 1)
                    return
                high_part(b, 0, g + 1, 1 - par)
                square(b, p, q)
                if not first:
                    kv_std(b, p - 1, (q + 3) % 4)
                ones_in_k(b, p, q)
                square(b, p + 1, q + 1)
                kv_std(b, p, q)
                ones_in_k(b, p + 1, q + 1)

            def high_mix(b):
                act.wait_ge(mix_dve, 6 * b + 5)
                for m in (2, 0, 1):
                    rows = slice(0, P) if m < 2 else slice(0, 64)
                    act.activation(m_hi[rows, m, :].rearrange("p (j d) -> p j d", j=CH), m_ps[rows, m, :, 0:P],
                                   ACT.Identity, bias=mmean[rows, m:m + 1]).then_inc(mix_act, 1)

            def normalise_out(b, g, par):
                Gn = GROUPS * b + g
                act.wait_ge(ovar_ready, Gn + 1)
                act.activation(ostd[:, par, :], omv[:, par, :, 1], ACT.Sqrt, bias=eps[:, 2:3]).then_inc(ostd_ready, 1)
                act.wait_ge(orstd_ready, Gn + 1)
                if not (isinstance(g, int) and g < 2):
                    act.wait_ge(t_ready, Gn - 1)
                for t in range(GTILES):
                    ins = act.activation(z[par][:, t, :], o_ps[par][:, t, :], ACT.Copy, scale=orstd[:, par, t:t + 1])
                ins.then_inc(z_ready, 1)

            def gain_bias(b, g, par):
                Gn = GROUPS * b + g
                act.wait_ge(t_ready, Gn + 1)
                if not (isinstance(g, int) and g < 2):
                    act.wait_ge(y_ready, Gn - 1)
                for c in range(CH):
                    ins = act.activation(wout[par][:, c, :], t_ps[par][:, c, :], ACT.Identity,
                                         bias=cols[:, 4, c:c + 1], scale=cols[:, 3, c:c + 1])
                ins.then_inc(w_ready, 1)

            def phase2_group(b, g, par, slot):
                if not (isinstance(g, int) and g >= GROUPS - 2):
                    high_part(b, 1, g + 2, par)
                if not (isinstance(g, int) and g < 2):
                    gain_bias(b, g - 2, par)
                normalise_out(b, g, par)

            with act.Fori(0, B) as b:
                act.wait_ge(gn_pe, 2 * b + 2)
                act.activation(gstd[:], ps[:, 0, 2:2 + CH], ACT.Sqrt, bias=eps[:, 0:1]).then_inc(gn_act, 1)
                high_part(b, 0, 0, 0)
                sweep(act, phase1_group, b)
                high_part(b, 1, 0, 0)
                high_part(b, 1, 1, 1)
                high_mix(b)
                sweep(act, phase2_group, b, head=4)
                gain_bias(b, GROUPS - 2, 0)
                gain_bias(b, GROUPS - 1, 1)

        @block.gpsimd
        def _(pool):
            pool.wait_ge(max_ready, 1)
            pool.partition_all_reduce(max_all[:], max_in[:], P, bass.bass_isa.ReduceOp.max).then_inc(setup_pool, 1)

            def scale_pair(b, p, q):
                Pn = PAIRS * b + p
                pool.wait_ge(rstd_ready, Pn + 1)
                r = rstd[:, q, :].rearrange("p (t a h) -> p t a h", t=2, a=2)
                k = kv[q][:, :, 0:C].rearrange("p t (h d) -> p t h d", d=DK)[:, :, :, 0:DK - 1]
                ins = pool.tensor_tensor(k, k, r[:, :, 0, :].unsqueeze(3).broadcast_to([P, 2, HEADS, DK - 1]), ALU.mult)
                if not (isinstance(p, int) and p >= PAIRS - 3):
                    v = kv[q][:, :, C + 1:2 * C + 1].rearrange("p t (h d) -> p t h d", d=DK)
                    ins = pool.tensor_tensor(v, v, r[:, :, 1, :].unsqueeze(3).broadcast_to([P, 2, HEADS, DK]), ALU.mult)
                ins.then_inc(scaled, 1)

            def low_part(b, g, par):
                H = 2 * GROUPS * b + GROUPS + g
                pool.wait_ge(hi_ready, H + 1)
                wait_parts_free(pool, b, 1, g)
                pool.tensor_tensor(lo[par][:], u[par][:], hi[par][:], ALU.subtract).then_inc(lo_ready, 1)

            def residual(b, g, par, s):
                Gn = GROUPS * b + g
                pool.wait_ge(w_ready, Gn + 1)
                xg, add = in_ring(s), wout[par]
                if isinstance(g, int) and GROUPS - 5 <= g < GROUPS - 2:
                    pool.wait_ge(late_added, 3 * b + g - (GROUPS - 5) + 1)
                    xg, add = xg[:, 0, :], add[:, 0, :]
                pool.tensor_tensor(xg, xg, add, ALU.add).then_inc(y_ready, 1)

            def phase2_group(b, g, par, slot):
                if not (isinstance(g, int) and g >= GROUPS - 2):
                    low_part(b, g + 2, par)
                if not (isinstance(g, int) and g < 2):
                    residual(b, g - 2, par, slot(-2))

            def ones_beside_v():
                one = eps[:, 3:4].unsqueeze(1).broadcast_to([P, 4, 1])
                for i in range(2):
                    ins = pool.tensor_tensor(kv[i][:].rearrange("p t (a c) -> p (t a) c", a=2)[:, :, C:C + 1],
                                             one, one, ALU.mult)
                ins.then_inc(kv_free, 1)

            with pool.Fori(0, B) as b:
                for q in range(4):
                    scale_pair(b, q, q)
                with pool.Fori(1, PAIRS // 4 - 1) as i:
                    for q in range(4):
                        scale_pair(b, 4 * i + q, q)
                for q in range(4):
                    scale_pair(b, PAIRS - 4 + q, q)
                low_part(b, 0, 0)
                low_part(b, 1, 1)
                sweep(pool, phase2_group, b, tail=4)
                slot = slots_from(pool, GROUPS * b, 2)
                residual(b, GROUPS - 2, 0, slot(GROUPS - 2))
                residual(b, GROUPS - 1, 1, slot(GROUPS - 1))
                pool.wait_ge(y_ready, GROUPS * b + GROUPS)
                ones_beside_v()

        @block.tensor
        def _(pe):
            pe.wait_ge(params_loaded, 16 * 14)
            for c in range(CH):
                for i, w in enumerate((wk_in, wv_in)):
                    for j in range(CH):
                        mm = pe.transpose(ps[:, c, i * C + j * P:i * C + (j + 1) * P], w[:, j, c * P:(c + 1) * P], ident)
            mm.then_inc(setup_pe, 1)
            pe.wait_ge(wc_ready, 1)
            pe.matmul(ps[:, 2, 0:C], pos[:, 1, :], wc[:, 1, 0:C], start=True, stop=True)
            for h in range(2):
                for d in range(2):
                    mm = pe.matmul(ps[d * HALF:(d + 1) * HALF, 3 + h, 0:C], pos[:, 0, h * HALF:(h + 1) * HALF],
                                   wc[:, 0, 0:C], start=True, stop=True)
            mm.then_inc(setup_pe, 1)
            pe.wait_ge(lmat_ready, 1)
            for j in range(CH):
                pe.matmul(ps[:, 5 + j, 0:C], lmat[:, j, :], wq_in[:, j, :], start=True, stop=True)
                mm = pe.matmul(ps[:, 5 + j, C:C + P], lmat[:, j, :], bq_rep[:, j, :], start=True, stop=True)
            mm.then_inc(setup_pe, 1)

            def keep_clock(n, bank):
                for _ in range(n):
                    pe.matmul(ps[:, bank, :], wkv_hi[:, 0, 0:P], wkv_hi[:, 0, :], start=True, stop=True)

            def project(t, par, out, sel_at, half, before_low=lambda: None):
                px = slice(t * W, (t + 1) * W)
                if isinstance(sel_at, int):
                    s, r = sel[:, sel_at:sel_at + 1], rowpart[:, half, :]
                else:
                    s = sel[:, bass.ds(sel_at, 1)]
                    r = rowpart[:, bass.ds(half, 1), :].rearrange("p a c -> p (a c)")
                pe.matmul(out, hi[par][:, 0, px], wkv_hi[:, 0, :], start=True, stop=False)
                pe.matmul(out, hi[par][:, 0, px], wkv_lo[:, 0, :], start=False, stop=False)
                pe.matmul(out[:, 0:C], s.broadcast_to([P, P]), r, start=False, stop=False, skip_group_check=True)
                pe.matmul(out, hi[par][:, 1, px], wkv_hi[:, 1, :], start=False, stop=False)
                pe.matmul(out, hi[par][:, 1, px], wkv_lo[:, 1, :], start=False, stop=False)
                before_low()
                pe.matmul(out, lo[par][:, 0, px], wkv_hi[:, 0, :], start=False, stop=False)
                return pe.matmul(out, lo[par][:, 1, px], wkv_hi[:, 1, :], start=False, stop=True)

            def project_pair(b, g, h, par, sel_at, half):
                Pn = PAIRS * b + 2 * g + h
                H = 2 * GROUPS * b + g
                start = isinstance(g, int) and g == 0 and h == 0
                if start:
                    pe.wait_ge(hi_ready, H + 1)
                elif h == 0:
                    pe.wait_ge(lo_ready, H + 1)
                if not (isinstance(g, int) and g == 0):
                    pe.wait_ge(kv_evac, Pn - 1)
                for t in range(2):
                    low_wait = (lambda: pe.wait_ge(lo_ready, H + 1)) if start and t == 0 else (lambda: None)
                    mm = project(2 * h + t, par, kv_ps[h][:, t, :], sel_at + 2 * h + t, half, low_wait)
                mm.then_inc(kv_proj, 1)

            def scores(b, p, q):
                Pn = PAIRS * b + p
                pe.wait_ge(scaled, Pn + 1)
                if isinstance(p, int) and p >= PAIRS - 3:
                    pe.wait_ge(last_v_scaled, 3 * b + p - (PAIRS - 4))
                pe.wait_ge(k_ones, Pn + 1)
                for t in range(2):
                    for j in range(CH):
                        v0 = C + j * (P + 1)
                        mm = pe.matmul(s_ps[j], kv[q][:, t, j * P:(j + 1) * P], kv[q][:, t, v0:v0 + P + 1],
                                       start=False, stop=False, skip_group_check=True)
                mm.then_inc(scored, 1)

            def phase1_group(b, g, par, slot):
                q = 2 * par
                score = not (isinstance(g, int) and g < 2)
                if score:
                    scores(b, 2 * g - 4, q)
                sel_at, half = (GTILES * g) % HALF, (GTILES * g) // HALF
                if not isinstance(g, int):
                    sel_at, half = pe.snap(sel_at), pe.snap(half)
                project_pair(b, g, 0, par, sel_at, half)
                if score:
                    scores(b, 2 * g - 3, q + 1)
                project_pair(b, g, 1, par, sel_at, half)
                if isinstance(g, int) and g == 1:
                    pe.wait_ge(kv_free, b + 1)
                    for j in range(CH):
                        pe.matmul(s_ps[j], zero16[:, 0:P], zero16[:], start=True, stop=False, skip_group_check=True)

            def project_out(b, g, par):
                H = 2 * GROUPS * b + GROUPS + g
                Gn = GROUPS * b + g
                pe.wait_ge(lo_ready, H + 1)
                if not (isinstance(g, int) and g < 2):
                    pe.wait_ge(z_ready, Gn - 1)
                for t in range(GTILES):
                    px = slice(t * W, (t + 1) * W)
                    out = o_ps[par][:, t, :]
                    first = True
                    for c in range(CH):
                        for st, m in ((hi, m_hi), (hi, m_lo), (lo, m_hi)):
                            pe.matmul(out, st[par][:, c, px], m[:, c, :], start=first, stop=False)
                            first = False
                    mm = pe.matmul(out, ones_hl[:], m_hi[:, 2, :], start=False, stop=True)
                mm.then_inc(o_ready, 1)
                return mm

            def transpose_back(b, g, par):
                Gn = GROUPS * b + g
                pe.wait_ge(z_ready, Gn + 1)
                if not (isinstance(g, int) and g < 2):
                    pe.wait_ge(w_ready, Gn - 1)
                for t in range(GTILES):
                    for c in range(CH):
                        mm = pe.transpose(t_ps[par][:, c, t * W:(t + 1) * W], z[par][:, t, c * P:(c + 1) * P], ident)
                mm.then_inc(t_ready, 1)

            def phase2_group(b, g, par, slot):
                project_out(b, g, par)
                if not (isinstance(g, int) and g < 2):
                    transpose_back(b, g - 2, par)

            pe.wait_ge(ring_free, 1)
            with pe.Fori(0, B) as b:
                keep_clock(5, 3)
                pe.wait_ge(gn_dve, 8 * b + 1)
                pe.matmul(ps[:, 0, 0:CH], const("blk8"), mv[:, :, 0], start=True, stop=True).then_inc(gn_pe, 1)
                keep_clock(1, 3)
                pe.wait_ge(gn_dve, 8 * b + 5)
                pe.matmul(ps[:, 0, 2:2 + CH], const("blk8"), gvar[:], start=True, stop=True).then_inc(gn_pe, 1)
                keep_clock(11, 3)
                sweep(pe, phase1_group, b)
                for p in range(PAIRS - 4, PAIRS):
                    scores(b, p, p % 4)
                    if p < PAIRS - 2:
                        keep_clock(2, 7)
                for j in range(CH):
                    mm = pe.matmul(s_ps[j], zero16[:, 0:P], zero16[:], start=False, stop=True, skip_group_check=True)
                mm.then_inc(sums_done, 1)
                keep_clock(8, 7)
                pe.wait_ge(mix_dve, 6 * b + 4)
                for m in range(3):
                    for j in range(CH):
                        st = wql[:, j, m * P:(m + 1) * P] if m < 2 else bql[:, j, :]
                        mm = pe.matmul(m_ps[:, m, j, 0:P + 1], st, sprime[:, j, :], start=True, stop=True)
                mm.then_inc(mix_pe, 1)
                keep_clock(10, 7)
                pe.wait_ge(mix_dve, 6 * b + 6)
                sweep(pe, phase2_group, b, head=4)
                transpose_back(b, GROUPS - 2, 0)
                keep_clock(8, 1)
                transpose_back(b, GROUPS - 1, 1)


def _constants():
    import numpy as np
    f = np.float32
    out = np.zeros((P, NCONST), f)

    def put(name, a):
        out[:, CAT[name][0]:CAT[name][1]] = a
    put("ident", np.eye(P, dtype=f))
    same = np.kron(np.eye(P // DK, dtype=f), np.ones((DK, DK), f))
    put("mask", same)
    put("blk8", np.kron(np.eye(P // 8, dtype=f), np.full((8, 8), 0.125, f)))
    rot = np.eye(DK, dtype=f)
    rot[DK - 1, :] = -1
    rot[:, DK - 1] = 0
    one = np.zeros((DK, DK), f)
    one[:, DK - 1] = 1
    put("lrot", np.kron(np.eye(P // DK, dtype=f), rot))
    put("lone", np.kron(np.eye(P // DK, dtype=f), one))
    half = C // 2
    t = (np.arange(1, W + 1, dtype=f) / f(W + 1e-6) * f(2.0 * np.pi)).astype(f)
    dim = np.arange(half, dtype=f)
    dim = (f(10000.0) ** (f(2.0) * np.floor(dim / f(2.0)) / f(half))).astype(f)
    a = (t[None, :] / dim[:, None]).astype(f)
    feat = np.where(np.arange(half)[:, None] % 2 == 0, np.sin(a), np.cos(a)).astype(f)
    put("pos", np.concatenate([feat, feat], axis=1))
    p = np.arange(P)
    put("sel", (p[:, None] % HALF == np.arange(HALF)[None, :]).astype(f))
    put("ones", np.repeat(((p == 0) | (p == 32)).astype(f)[:, None], P, axis=1))
    return out


_INS = ["x", "L0_conv_Wq", "L0_conv_bq", "L0_conv_Wk", "L0_conv_bk", "L0_conv_Wv", "L0_conv_bv", "L0_conv_gK",
        "L0_conv_bK", "L0_conv_gV", "L0_conv_bV", "L0_conv_g_ln", "L0_conv_b_ln"]


def kernel(**inputs):
    import numpy as _np
    import concourse.bacc as _bacc
    from concourse import mybir as _mybir
    from concourse.bass_utils import run_bass_kernel_spmd as _run

    nc = _bacc.Bacc("TRN2", target_bir_lowering=False, num_devices=1)
    arrays, args = {}, []
    for name in _INS:
        a = _np.ascontiguousarray(inputs[name])
        arrays[f"in_{name}_dram"] = a
        args.append(nc.dram_tensor(f"in_{name}_dram", a.shape, _mybir.dt.from_np(a.dtype), kind="ExternalInput").ap())
    arrays["consts_dram"] = _constants()
    args.append(nc.dram_tensor("consts_dram", (P, NCONST), _mybir.dt.float32, kind="ExternalInput").ap())
    args.append(nc.dram_tensor("out_0_dram", (B, C, ROWS, W), _mybir.dt.float32, kind="ExternalOutput").ap())
    build(nc, *args)
    r = _run(nc, [arrays], core_ids=[0])
    return r.results[0]["out_0_dram"]
```
